# Optimizing a Trainium2 kernel written in Bass

```python
import numpy as np
import jax
import jax.numpy as jnp

def _softmax(x, axis=-1):
    return jax.nn.softmax(x, axis=axis)

def _gelu(x):
    return jax.nn.gelu(x, approximate=True)

def _silu(x):
    return jax.nn.silu(x)

def _sigmoid(x):
    return jax.nn.sigmoid(x)

def _layernorm(x, axis=-1, eps=1e-05):
    m = jnp.mean(x, axis=axis, keepdims=True)
    v = jnp.var(x, axis=axis, keepdims=True)
    return (x - m) / jnp.sqrt(v + eps)

def _scatter_add(tgt, idx, src, axis=0):
    return tgt.at[idx].add(src)

def _segment_sum(src, seg, n):
    return jax.ops.segment_sum(src, seg, n)
kernel_name = 'mk_macaron_d1_jaxref_r8_10ee32'

def setup_inputs(seed: int=0):
    np.random.seed(seed)
    _w = jnp.asarray

    def _L0_attn_setup():
        import jax, jax.numpy as jnp
        import numpy as np
        HEADS = 16
        DIM_HEAD = 64
        B, T, C = (4, 256, 128)

        def apply_rope(x):
            d = x.shape[-1]
            seq_len = x.shape[1]
            inv_freq = 1.0 / 10000.0 ** (jnp.arange(0, d, 2, dtype=jnp.float32) / d)
            pos = jnp.arange(seq_len, dtype=jnp.float32)
            ang = pos[:, None] * inv_freq[None, :]
            sin = jnp.sin(ang)[None]
            cos = jnp.cos(ang)[None]
            x1, x2 = (x[..., 0::2], x[..., 1::2])
            rot = jnp.stack([x1 * cos - x2 * sin, x1 * sin + x2 * cos], axis=-1)
            return rot.reshape(x.shape)
        key = jax.random.key(seed)
        ks = jax.random.split(key, 6)
        inner = HEADS * DIM_HEAD
        w = 0.02
        return {'x': jax.random.normal(ks[0], (B, T, C), dtype=jnp.float32), 'Wq': jax.random.normal(ks[1], (C, inner), dtype=jnp.float32) * w, 'Wk': jax.random.normal(ks[2], (C, inner), dtype=jnp.float32) * w, 'Wv': jax.random.normal(ks[3], (C, inner), dtype=jnp.float32) * w, 'Wo': jax.random.normal(ks[4], (inner, C), dtype=jnp.float32) * w, 'bo': jnp.zeros((C,), dtype=jnp.float32)}
    _L0_attn_in = _L0_attn_setup()

    def _L0_ffn_setup():
        import jax, jax.numpy as jnp
        import numpy as np
        B, S, D = (4, 256, 128)
        E, F = (8, 512)
        key = jax.random.key(seed)
        ks = jax.random.split(key, 5)
        x = jax.random.normal(ks[0], (B, S, D), dtype=jnp.float32)
        switch_w = jax.random.normal(ks[1], (D, E), dtype=jnp.float32) * D ** (-0.5)
        switch_b = jnp.zeros((E,), dtype=jnp.float32)
        w1 = jax.random.normal(ks[2], (E, D, F), dtype=jnp.float32) * D ** (-0.5)
        b1 = jnp.zeros((E, F), dtype=jnp.float32)
        w2 = jax.random.normal(ks[3], (E, F, D), dtype=jnp.float32) * F ** (-0.5)
        b2 = jnp.zeros((E, D), dtype=jnp.float32)
        return {'x': x, 'switch_w': switch_w, 'switch_b': switch_b, 'w1': w1, 'b1': b1, 'w2': w2, 'b2': b2}
    _L0_ffn_in = _L0_ffn_setup()
    _d = {'L0_attn_x': _L0_attn_in['x'], 'L0_attn_Wq': _L0_attn_in['Wq'], 'L0_attn_Wk': _L0_attn_in['Wk'], 'L0_attn_Wv': _L0_attn_in['Wv'], 'L0_attn_Wo': _L0_attn_in['Wo'], 'L0_attn_bo': _L0_attn_in['bo'], 'L0_ffn_switch_w': _L0_ffn_in['switch_w'], 'L0_ffn_switch_b': _L0_ffn_in['switch_b'], 'L0_ffn_w1': _L0_ffn_in['w1'], 'L0_ffn_b1': _L0_ffn_in['b1'], 'L0_ffn_w2': _L0_ffn_in['w2'], 'L0_ffn_b2': _L0_ffn_in['b2']}
    _x0 = _d['L0_attn_x']
    _d['L0_attn_x'] = jax.random.normal(jax.random.fold_in(jax.random.key(seed), 1), (8, 512, 128), dtype=_x0.dtype)
    del _x0
    return _d

def reference(L0_attn_x, L0_attn_Wq, L0_attn_Wk, L0_attn_Wv, L0_attn_Wo, L0_attn_bo, L0_ffn_switch_w, L0_ffn_switch_b, L0_ffn_w1, L0_ffn_b1, L0_ffn_w2, L0_ffn_b2):

    def _L0_attn_ref(x, Wq, Wk, Wv, Wo, bo):
        import jax, jax.numpy as jnp
        import numpy as np
        HEADS = 16
        DIM_HEAD = 64
        B, T, C = (4, 256, 128)

        def apply_rope(x):
            d = x.shape[-1]
            seq_len = x.shape[1]
            inv_freq = 1.0 / 10000.0 ** (jnp.arange(0, d, 2, dtype=jnp.float32) / d)
            pos = jnp.arange(seq_len, dtype=jnp.float32)
            ang = pos[:, None] * inv_freq[None, :]
            sin = jnp.sin(ang)[None]
            cos = jnp.cos(ang)[None]
            x1, x2 = (x[..., 0::2], x[..., 1::2])
            rot = jnp.stack([x1 * cos - x2 * sin, x1 * sin + x2 * cos], axis=-1)
            return rot.reshape(x.shape)
        b, t, c = x.shape
        h, d = (HEADS, DIM_HEAD)
        scale = d ** (-0.5)

        def split_heads(z):
            return z.reshape(b, t, h, d).transpose(0, 2, 1, 3).reshape(b * h, t, d)
        q = split_heads(x @ Wq)
        k = split_heads(x @ Wk)
        v = split_heads(x @ Wv)
        q = apply_rope(q)
        k = apply_rope(k)
        sim = jnp.einsum('bid,bjd->bij', q, k) * scale
        causal = jnp.tril(jnp.ones((t, t), dtype=bool))
        sim = jnp.where(causal[None], sim, -jnp.inf)
        attn = jax.nn.softmax(sim, axis=-1)
        out = jnp.einsum('bij,bjd->bid', attn, v)
        out = out.reshape(b, h, t, d).transpose(0, 2, 1, 3).reshape(b, t, h * d)
        return out @ Wo + bo

    def _L0_ffn_ref(x, switch_w, switch_b, w1, b1, w2, b2):
        import jax, jax.numpy as jnp
        import numpy as np
        B, S, D = (4, 256, 128)
        E, F = (8, 512)
        b, s, d = x.shape
        t = x.reshape(-1, d)
        logits = t @ switch_w + switch_b
        route_prob = jax.nn.softmax(logits, axis=-1)
        route_prob_max = jnp.max(route_prob, axis=-1)
        routes = jnp.argmax(route_prob, axis=-1)
        out = jnp.zeros_like(t)
        n_experts = w1.shape[0]
        for e in range(n_experts):
            h = jax.nn.gelu(t @ w1[e] + b1[e])
            y = h @ w2[e] + b2[e]
            mask = (routes == e)[:, None]
            out = jnp.where(mask, y, out)
        out = out * route_prob_max[:, None]
        return out.reshape(b, s, d)
    x = L0_attn_x
    x = x + 0.5 * _L0_ffn_ref(_layernorm(x, axis=-1), L0_ffn_switch_w, L0_ffn_switch_b, L0_ffn_w1, L0_ffn_b1, L0_ffn_w2, L0_ffn_b2)
    x = x + _L0_attn_ref(_layernorm(x, axis=-1), L0_attn_Wq, L0_attn_Wk, L0_attn_Wv, L0_attn_Wo, L0_attn_bo)
    x = x + 0.5 * _L0_ffn_ref(_layernorm(x, axis=-1), L0_ffn_switch_w, L0_ffn_switch_b, L0_ffn_w1, L0_ffn_b1, L0_ffn_w2, L0_ffn_b2)
    return x

_drawn_inputs = setup_inputs


def setup_inputs(seed=0):
    import zlib

    import numpy as np

    out = dict(_drawn_inputs(seed))
    spreads = {'L0_attn_bo': (0.0, 0.1),
     'L0_ffn_switch_b': (0.0, 0.1),
     'L0_ffn_b1': (0.0, 0.297),
     'L0_ffn_b2': (0.0, 0.1)}
    factors = {'L0_attn_Wq': 8.0, 'L0_attn_Wk': 8.0, 'L0_attn_Wv': 3.143, 'L0_attn_Wo': 2.935}
    for name, (base, spread) in spreads.items():
        noise = np.random.default_rng([zlib.crc32(name.encode()), seed]).standard_normal(out[name].shape)
        drawn = base * np.exp(spread * noise) if base else spread * noise
        out[name] = jnp.asarray(drawn.astype(out[name].dtype))
    for name, factor in factors.items():
        out[name] = (out[name] * factor).astype(out[name].dtype)
    return out
```

```python
from contextlib import ExitStack

import numpy as np

import concourse.bass as bass
from concourse import mybir

B, T, D = 8, 512, 128
TILE = 128
NJ = T // TILE
N = B * T
HEADS, DH = 16, 64
PAIRS = HEADS // 2
EX, F = 8, 512
FC = F // 128
RING = 8
SLOTS = -(-(N // TILE + EX - 1) // RING) * RING
REGION = N + TILE
SPARE = SLOTS - N // TILE
ROWS = EX * REGION + SPARE * TILE
XN, XX, GATE, TOK, ROW = 0, D, 2 * D, 2 * D + 1, 2 * D + 2
NOWHERE = 1 << 20
EPS = 1e-5
MASKED = -1e30
SUPER = [[(3, 0, 4)], [(0, 0, 1), (2, 128, 3)], [(1, 0, 2)]]
NG = 2 * len(SUPER)


def macaron_kernel(nc, x, wq, wk, wv, wo, bo, sw, sb_, w1, b1, w2, b2,
                   c_ident, c_mask, c_upper, c_rope, c_small, c_slots, out):
    f32, f32r, bf16, i32 = mybir.dt.float32, mybir.dt.float32r, mybir.dt.bfloat16, mybir.dt.int32
    ALU, ACT, AX = mybir.AluOpType, mybir.ActivationFunctionType, mybir.AxisListType
    ds = bass.ds
    ctx = ExitStack()
    with ctx:
        def sb(name, shape, dt=f32):
            return ctx.enter_context(nc.sbuf_tensor(name, shape, dt))

        def sem(name):
            return ctx.enter_context(nc.semaphore(name))

        region = nc.dram_tensor("routed_rows", [ROWS, ROW], f32).ap()
        x1 = nc.dram_tensor("x_after_ffn1", [N, D], f32).ap()

        ident = sb("ident", [128, 128])
        identb = sb("identb", [128, 128], bf16)
        maskb = sb("maskb", [128, 128], bf16)
        upperb = sb("upperb", [128, 128], bf16)
        onesb = sb("onesb", [128, 128], bf16)
        onesr = sb("onesr", [2, 128], f32r)
        rope = sb("rope", [128, 4, T])
        small = sb("small", [128, 2, NJ, EX])
        sbias = sb("sbias", [128, NJ, EX])
        slot_c = sb("slot_c", [1, SLOTS + SLOTS * EX + EX * EX + EX * 32])
        tokens = sb("tokens", [128, N // TILE], i32)
        bo_bc = sb("bo_bc", [128, D])
        swt = sb("swt", [128, EX])
        w1s = sb("w1s", [128, 2, EX * F], f32r)
        w2s = sb("w2s", [128, EX, FC, D])
        b1s = sb("b1s", [2, EX * F], f32r)
        b2s = sb("b2s", [2, EX * D], f32r)
        wqk = sb("wqk", [128, 4, HEADS * DH], f32r)
        wvs = sb("wvs", [128, 2, HEADS * DH], f32r)
        wos = sb("wos", [128, PAIRS, D])
        xnT = sb("xnT", [128, 2, N], f32r)

        raw = [sb(f"raw{i}", [128, 512]) for i in range(2)]
        bias_hl = sb("bias_hl", [128, 2, 40], f32r)
        bias_raw = sb("bias_raw", [128, 40])
        PL = [sb(f"payload{i}", [128, NJ, ROW]) for i in range(2)]
        pad = sb("pad", [128, ROW])
        stats = sb("stats", [128, NJ, 6])
        mv = sb("mv", [128, NJ, 2])
        var = sb("var", [128, NJ])
        rstd = sb("rstd", [128, NJ])
        mhalf = sb("mhalf", [128, NJ])
        xT = sb("xT", [128, T])
        lg = sb("lg", [128, NJ, EX])
        lmax = sb("lmax", [128, NJ])
        ldiff = sb("ldiff", [128, NJ, EX])
        lexp = sb("lexp", [128, NJ, EX])
        lsum = sb("lsum", [128, NJ])
        eq = sb("eq", [128, NJ, EX])
        first = sb("first", [128, NJ])
        oh = sb("oh", [128, NJ, EX])
        ohb = sb("ohb", [128, NJ, EX], bf16)
        ohsum = sb("ohsum", [128, EX])
        cum = sb("cum", [128, EX])
        cumb = sb("cumb", [128, EX], bf16)
        rk = sb("rk", [128, NJ, EX])
        posf = sb("posf", [128, NJ])
        pos = [sb(f"pos{i}", [128, NJ], i32) for i in range(2)]
        cnt = sb("cnt", [1, EX])
        tiles_e = sb("tiles_e", [1, EX])
        tri = sb("tri", [1, EX, EX])
        ends = sb("ends", [1, EX])
        skip = sb("skip", [1, EX])
        sl_e = sb("sl_e", [1, SLOTS])
        sl_r = sb("sl_r", [1, SLOTS])
        slot_expert = sb("slot_expert", [1, SLOTS], i32)
        slot_row = sb("slot_row", [1, SLOTS], i32)
        pad_row = sb("pad_row", [1, EX], i32)
        QT = [sb(f"qT{i}", [128, T]) for i in range(2)]
        KT = [sb(f"kT{i}", [128, T]) for i in range(2)]
        cosq, sinq, cosk, sink = [sb(n, [128, T]) for n in ("x_cosq", "x_sinq", "x_cosk", "x_sink")]
        P = [sb(f"P{i}", [128, 512]) for i in range(3)]
        ge, ge2 = [P[i][0:1, 0:SLOTS * EX].rearrange("p (s e) -> p s e", e=EX) for i in range(2)]
        cmp32 = P[2][0:1, 0:EX * 32].rearrange("p (e s) -> p e s", s=32)
        PT = [sb(f"PT{i}", [128, 512]) for i in range(2)]
        V = [sb(f"V{i}", [128, NJ, 128]) for i in range(2)]
        O = [sb(f"O{i}", [128, NJ, 2, DH]) for i in range(2)]
        OT = sb("OT", [128, T])
        WS = [sb(f"WS{i}", [128, 4, 128], f32r) for i in range(2)]
        xTb = sb("xTb", [128, 2, T], f32r)
        nmax = [sb(f"nmax{i}", [128, 8]) for i in range(2)]
        rsum = [sb(f"rsum{i}", [128, 8]) for i in range(2)]
        rinv = sb("rinv", [128, 8])
        flatV = [t[:, :, :].rearrange("p j d -> p (j d)") for t in V]
        flatO = [t[:, :, :, :].rearrange("p j h d -> p (j h d)") for t in O]
        XS = [t[:, 0:ROW] for t in (*QT, *KT, sinq, cosk, *flatV)]
        XH = [sb(f"xh{i}", [128, 128], f32r) for i in range(2)]
        XL = [sb(f"xl{i}", [128, 128], f32r) for i in range(2)]
        G = [P[0][:, :], P[1][:, :], P[2][:, :], flatO[0]]
        GT = [PT[0][:, :], PT[1][:, :], cosq[:, :], sink[:, :]]
        OUT = [OT[:, 128 * i:128 * i + 128] for i in range(4)]
        out_tok = [sb(f"out_tok{i}", [128, 1], i32) for i in range(4)]

        bank = [ctx.enter_context(nc.psum_tensor(f"bank{i}", [128, 512], f32)) for i in range(8)]
        bS, bT, bJ, bO, bY = bank[0:3], bank[3:5], bank[5], bank[6], bank[7]

        c_ld, raw_ld0, raw_ld1, raw_hi, raw_lo = [sem(n) for n in (
            "consts_loaded", "raw_loaded0", "raw_loaded1", "raw_high", "raw_low")]
        raw_ld = [raw_ld0, raw_ld1]
        prep, bias_hi, bias_lo, bias_ld, w2_ld = [sem(n) for n in (
            "prep", "bias_high", "bias_low", "bias_rows", "w2_loaded")]
        spare_st = sem("spare_rows_stored")
        x_ld = [sem("x_loaded0"), sem("x_loaded1")]
        r_sc = [sem("rows_scattered0"), sem("rows_scattered1")]
        r_var, r_rstd, r_xn, r_t, r_xt, r_lg, r_d, r_ex, r_oh, r_rk, r_pos, r_cnt, r_tab, r_pad = [sem("router_" + n) for n in (
            "var", "rstd", "normed", "transposed", "xT", "logits", "diff", "exp", "onehot", "rank", "pos", "counts", "table", "padded")]
        e_ld = [sem(f"tile_loaded{i}") for i in range(RING)]
        e_sc = [sem(f"tile_scattered{i}") for i in range(4)]
        e_tx, e_xs, e_h, e_g, e_gt, e_ge, e_y, e_o = [sem("expert_" + n) for n in (
            "xT", "xsplit", "hidden", "gelu", "hiddenT", "hiddenT_out", "y", "out")]
        l_t, l_hi, l_lo = [sem("ln_" + n) for n in ("transposed", "high", "low")]
        ws_ld = [sem("ws_loaded0"), sem("ws_loaded1")]
        xb_ld, tick, phase = sem("xTb_loaded"), sem("tick"), sem("phase")
        s_pq, s_pk, s_pv, s_qr, s_kr, s_vr, s_qv, s_kv, s_qt, s_kt = [sem("a_" + n) for n in (
            "proj_q", "proj_k", "proj_v", "q_read", "k_read", "v_read", "q_parts", "k_parts", "q_roped", "k_roped")]
        s_S, s_max, s_exp, s_T, s_pt, s_av, s_norm, s_ot, s_ote, s_wo, s_x2, s_bo = [sem("a_" + n) for n in (
            "scores", "max", "exp", "PT", "PT_out", "AV", "norm", "OT", "OT_out", "wo", "x2", "bo")]

        def wait(e, s, v):
            if not isinstance(v, int) or v > 0:
                e.wait_ge(s, v)

        def wait_here(e, s, v):
            wait(e, s, v)
            e.sem_inc(tick, 1)

        def all_meet(e, k):
            e.drain().then_inc(phase, 1)
            e.wait_ge(phase, 5 * k)

        chunks = [(w1[e], w1s[:, 0, e * F:(e + 1) * F], w1s[:, 1, e * F:(e + 1) * F]) for e in range(EX)]
        for w, dst, k in ((wq, wqk, 0), (wk, wqk, 2), (wv, wvs, 0)):
            for h in range(2):
                cols = slice(512 * h, 512 * h + 512)
                chunks.append((w[:, cols], dst[:, k, cols], dst[:, k + 1, cols]))
        NCH = len(chunks)

        def xrows(src, b):
            return src.rearrange("(b j p) d -> b p j d", p=TILE, j=NJ)[ds(b, 1)].rearrange("o p j d -> p (o j) d")

        def pool_rstd(e, m):
            e.wait_ge(r_var, m + 1)
            nc.gpsimd.tensor_tensor(rstd[:, :], var[:, :], mhalf[:, :], ALU.pow).then_inc(r_rstd, 1)

        def dve_norm(e, m, par):
            for j in range(NJ):
                nc.vector.bn_stats(stats[:, j, :], PL[par][:, j, XX:XX + D])
            nc.vector.drain()
            for j in range(NJ):
                nc.vector.bn_aggr(mv[:, j, :], stats[:, j, :])
            nc.vector.drain()
            nc.vector.tensor_scalar(var[:, :], mv[:, :, 1], EPS, None, ALU.add).then_inc(r_var, 1)
            e.wait_ge(r_rstd, m + 1)
            for j in range(NJ):
                last = nc.vector.tensor_scalar(PL[par][:, j, XN:XN + D], PL[par][:, j, XX:XX + D],
                                               mv[:, j, 0:1], rstd[:, j:j + 1], ALU.subtract, ALU.mult)
            last.then_inc(r_xn, 1)

        def pe_norm_T(par, bankT, done):
            for j in range(NJ):
                last = nc.tensor.transpose(bankT[:, 128 * j:128 * j + 128], PL[par][:, j, XN:XN + D], ident[:, :])
            last.then_inc(done, 1)

        def act_xT(e, n, bankT):
            e.wait_ge(r_t, n + 1)
            wait(e, r_lg, n)
            nc.scalar.activation(xT[:, :], bankT[:, :], ACT.Copy).then_inc(r_xt, 1)

        def pe_logits(e, n, bankL):
            e.wait_ge(r_xt, n + 1)
            for j in range(NJ):
                last = nc.tensor.matmul(bankL[:, EX * j:EX * j + EX], xT[:, 128 * j:128 * j + 128], swt[:, :],
                                        start=True, stop=True)
            last.then_inc(r_lg, 1)

        def dve_route(e, n, bankL):
            V_ = nc.vector
            e.wait_ge(r_lg, n + 1)
            V_.tensor_tensor(lg[:, :, :], bankL[:, 0:NJ * EX].rearrange("p (j e) -> p j e", j=NJ), sbias[:, :, :], ALU.add)
            V_.drain()
            V_.tensor_reduce(lmax[:, :], lg[:, :, :], AX.X, ALU.max)
            V_.drain()
            top = lmax[:, :].unsqueeze(2).broadcast_to([128, NJ, EX])
            V_.tensor_tensor(ldiff[:, :, :], lg[:, :, :], top, ALU.subtract).then_inc(r_d, 1)
            V_.tensor_tensor(eq[:, :, :], lg[:, :, :], top, ALU.is_equal)
            V_.drain()
            V_.tensor_tensor(eq[:, :, :], eq[:, :, :], small[:, 0], ALU.mult)
            V_.drain()
            V_.tensor_reduce(first[:, :], eq[:, :, :], AX.X, ALU.max)
            V_.drain()
            V_.tensor_tensor(oh[:, :, :], small[:, 0], first[:, :].unsqueeze(2).broadcast_to([128, NJ, EX]), ALU.is_equal)
            V_.drain()
            V_.tensor_copy(ohb[:, :, :], oh[:, :, :])
            V_.tensor_copy(cumb[:, :], cum[:, :]).then_inc(r_oh, 1)

        def act_exp(e, n):
            e.wait_ge(r_d, n + 1)
            nc.scalar.activation(lexp[:, :, :], ldiff[:, :, :], ACT.Exp).then_inc(r_ex, 1)

        def pe_rank(e, n, bankR):
            e.wait_ge(r_oh, n + 1)
            R = bankR[:, 0:NJ * EX]
            nc.tensor.matmul(R, onesb[:, :], cumb[:, :].unsqueeze(1).broadcast_to([128, NJ, EX]), start=True, stop=False)
            for j in range(NJ - 1):
                nc.tensor.matmul(bankR[:, EX * (j + 1):NJ * EX], onesb[:, :],
                                 ohb[:, j:j + 1, :].broadcast_to([128, NJ - 1 - j, EX]), start=False, stop=False)
            nc.tensor.matmul(R, upperb[:, :], ohb[:, :, :], start=False, stop=True).then_inc(r_rk, 1)

        def dve_position(e, n, b, par, bankR):
            V_ = nc.vector
            e.wait_ge(r_rk, n + 1)
            V_.tensor_tensor(rk[:, :, :], bankR[:, 0:NJ * EX].rearrange("p (j e) -> p j e", j=NJ), small[:, 1], ALU.add)
            V_.tensor_reduce(ohsum[:, :], oh[:, :, :].rearrange("p j e -> p e j"), AX.X, ALU.add)
            V_.drain()
            V_.tensor_tensor(rk[:, :, :], rk[:, :, :], oh[:, :, :], ALU.mult)
            V_.tensor_tensor(cum[:, :], cum[:, :], ohsum[:, :], ALU.add)
            V_.drain()
            V_.tensor_reduce(posf[:, :], rk[:, :, :], AX.X, ALU.add)
            e.wait_ge(r_ex, n + 1)
            V_.tensor_reduce(lsum[:, :], lexp[:, :, :], AX.X, ALU.add)
            V_.drain()
            V_.reciprocal(lsum[:, :], lsum[:, :])
            V_.tensor_copy(PL[par][:, :, TOK:TOK + 1].bitcast(i32).rearrange("p j o -> p (j o)"), tokens[:, ds(b * NJ, NJ)])
            V_.drain()
            V_.tensor_scalar(PL[par][:, :, GATE], lsum[:, :], 0.5, None, ALU.mult)
            V_.tensor_copy(pos[par][:, :], posf[:, :]).then_inc(r_pos, 1)

        def pool_scatter(e, n, par):
            wait_here(e, r_pos, n + 1)
            for j in range(NJ):
                nc.gpsimd.indirect_dma_start(region, bass.IndirectOffsetOnAxis(ap=pos[par][:, j:j + 1], axis=0),
                                             PL[par][:, j, :], None).then_inc(r_sc[par], 16)

        def pe_counts(e, k):
            e.wait_ge(r_cnt, 2 * k + 1)
            nc.tensor.matmul(bY[:, 0:EX], onesb[:, :], cumb[:, :], start=True, stop=True).then_inc(r_cnt, 1)

        def dve_table(e, k):
            V_ = nc.vector
            o = 0
            jota = slot_c[:, o:o + SLOTS]; o += SLOTS
            jb = slot_c[:, o:o + SLOTS * EX].rearrange("p (s e) -> p s e", e=EX); o += SLOTS * EX
            low = slot_c[:, o:o + EX * EX].rearrange("p (a c) -> p a c", c=EX); o += EX * EX
            steps = slot_c[:, o:o + EX * 32].rearrange("p (e s) -> p e s", s=32)
            V_.tensor_copy(cumb[:, :], cum[:, :]).then_inc(r_cnt, 1)
            e.wait_ge(r_cnt, 2 * k + 2)
            V_.tensor_copy(cnt[:, :], bY[0:1, 0:EX])
            V_.drain()
            V_.tensor_tensor(cmp32[:, :, :], steps, cnt[:, :].unsqueeze(2).broadcast_to([1, EX, 32]), ALU.is_lt)
            V_.tensor_tensor(skip[:, :], cnt[:, :], small[0:1, 1, 0, :], ALU.add)
            V_.drain()
            V_.tensor_copy(pad_row[:, :], skip[:, :])
            V_.tensor_reduce(tiles_e[:, :], cmp32[:, :, :], AX.X, ALU.add)
            V_.drain()
            V_.tensor_tensor(tri[:, :, :], low, tiles_e[:, :].unsqueeze(1).broadcast_to([1, EX, EX]), ALU.mult)
            V_.tensor_scalar(skip[:, :], tiles_e[:, :], -float(TILE), float(REGION), ALU.mult, ALU.add)
            V_.drain()
            V_.tensor_reduce(ends[:, :], tri[:, :, :], AX.X, ALU.add)
            V_.drain()
            V_.tensor_tensor(ge[:, :, :], jb, ends[:, :].unsqueeze(1).broadcast_to([1, SLOTS, EX]), ALU.is_ge)
            V_.drain()
            V_.tensor_reduce(sl_e[:, :], ge[:, :, :], AX.X, ALU.add)
            V_.tensor_tensor(ge2[:, :, :], ge[:, :, :], skip[:, :].unsqueeze(1).broadcast_to([1, SLOTS, EX]), ALU.mult)
            V_.drain()
            V_.tensor_reduce(sl_r[:, :], ge2[:, :, :], AX.X, ALU.add)
            V_.tensor_scalar(sl_e[:, :], sl_e[:, :], float(EX - 1), None, ALU.min)
            V_.drain()
            V_.tensor_tensor(sl_r[:, :], sl_r[:, :], jota, ALU.add)
            V_.tensor_copy(slot_expert[:, :], sl_e[:, :])
            V_.drain()
            V_.tensor_copy(slot_row[:, :], sl_r[:, :]).then_inc(r_tab, 1)

        def sp_pads(e, k, scattered):
            e.wait_ge(r_tab, k + 1)
            for par in range(2):
                wait(e, r_sc[par], scattered[par])
            for x_ in range(EX):
                row = nc.sync.value_load(pad_row[0:1, x_:x_ + 1], min_val=0, max_val=EX * REGION - TILE)
                e.dma_start(region[ds(row, TILE), :], pad[:, :]).then_inc(r_pad, 16)

        def stepped(engine, step, lag):
            for j in range(RING):
                step(j, j)
            with engine.Fori(1, SLOTS // RING - 1) as t:
                for s in range(RING):
                    step(t * RING + s, s)
            for j in range(SLOTS - RING, SLOTS + lag):
                step(j, j % RING)

        def tile_at(j, lo=0):
            return not isinstance(j, int) or lo <= j < SLOTS

        def uses(k, j, ring):
            return j // ring + (k * (SLOTS // ring) + 1)

        def expert_of(engine, j):
            return engine.value_load(slot_expert[0:1, ds(j, 1)], min_val=0, max_val=EX - 1)

        def experts_sp(e, k):
            e.wait_ge(r_pad, 16 * EX * (k + 1))
            if k == 0:
                e.wait_ge(spare_st, 16 * SPARE)
            def step(j, s):
                wait_here(e, e_o, k * SLOTS + j - (RING - 1))
                row = nc.sync.value_load(slot_row[0:1, ds(j, 1)], min_val=0, max_val=ROWS - TILE)
                e.dma_start(XS[s], region[ds(row, TILE), :]).then_inc(e_ld[s], 16)
            stepped(nc.sync, step, 0)

        def experts_pe(e, k):
            J = k * SLOTS
            def tx(j, s):
                e.wait_ge(e_ld[s], 16 * uses(k, j, RING))
                wait(e, e_xs, J + j)
                nc.tensor.transpose(bJ[:, 0:128], XS[s][:, XN:XN + D], ident[:, :]).then_inc(e_tx, 1)
            def hidden(j, s):
                ex = expert_of(nc.tensor, j)
                e.wait_ge(e_xs, J + j + 1)
                wait(e, e_g, J + j - 1)
                s = s % 2
                hi, lo = w1s[:, 0, ds(ex * F, F)], w1s[:, 1, ds(ex * F, F)]
                nc.tensor.matmul(bS[s][:, :], XH[s][:, :], hi, start=True, stop=False)
                nc.tensor.matmul(bS[s][:, :], XH[s][:, :], lo, start=False, stop=False)
                nc.tensor.matmul(bS[s][:, :], XL[s][:, :], hi, start=False, stop=False)
                nc.tensor.matmul(bS[s][:, :], onesr[:, :], b1s[:, ds(ex * F, F)], start=False, stop=True).then_inc(e_h, 1)
            def hidden_T(j, s):
                e.wait_ge(e_g, J + j + 1)
                wait(e, e_ge, J + j - 1)
                for c in range(FC):
                    last = nc.tensor.transpose(bT[s % 2][:, 128 * c:128 * c + 128], G[s % 4][:, 128 * c:128 * c + 128],
                                               ident[:, :])
                last.then_inc(e_gt, 1)
            def down(j, s):
                ex = expert_of(nc.tensor, j)
                e.wait_ge(e_ge, J + j + 1)
                wait(e, e_o, J + j)
                for c in range(FC):
                    nc.tensor.matmul(bY[:, 0:D], GT[s % 4][:, 128 * c:128 * c + 128],
                                     w2s[:, ds(ex, 1), c, :].rearrange("p o d -> p (o d)"), start=(c == 0), stop=False)
                nc.tensor.matmul(bY[:, 0:D], onesr[:, :], b2s[:, ds(ex * D, D)], start=False, stop=True).then_inc(e_y, 1)
            tx(0, 0)
            def step(j, s):
                if not isinstance(j, int) or j + 1 < SLOTS:
                    tx(j + 1, (s + 1) % RING)
                if tile_at(j):
                    hidden(j, s)
                if tile_at(j - 1):
                    hidden_T(j - 1, (s - 1) % RING)
                if tile_at(j - 2):
                    down(j - 2, (s - 2) % RING)
            stepped(nc.tensor, step, 2)

        def experts_dve(e, k):
            J = k * SLOTS
            def split(j, s):
                e.wait_ge(e_tx, J + j + 1)
                wait(e, e_h, J + j - 1)
                nc.vector.tensor_copy(XH[s % 2][:, :], bJ[:, 0:128])
                nc.vector.drain()
                nc.vector.tensor_tensor(XL[s % 2][:, :], bJ[:, 0:128], XH[s % 2][:, :], ALU.subtract).then_inc(e_xs, 1)
            def last(j, s):
                e.wait_ge(e_y, J + j + 1)
                if k or not isinstance(j, int) or j >= 4:
                    e.wait_ge(e_sc[s % 4], 16 * (uses(k, j, 4) - 1))
                nc.vector.tensor_copy(out_tok[s % 4][:, :], XS[s][:, TOK:TOK + 1].bitcast(i32))
                nc.vector.scalar_tensor_tensor(OUT[s % 4], bY[:, 0:D], XS[s][:, GATE:GATE + 1], XS[s][:, XX:XX + D],
                                               ALU.mult, ALU.add).then_inc(e_o, 1)
            split(0, 0)
            def step(j, s):
                if not isinstance(j, int) or j + 1 < SLOTS:
                    split(j + 1, (s + 1) % RING)
                if tile_at(j - 2):
                    last(j - 2, (s - 2) % RING)
            stepped(nc.vector, step, 2)

        def experts_act(e, k):
            J = k * SLOTS
            def step(j, s):
                if tile_at(j):
                    e.wait_ge(e_h, J + j + 1)
                    wait(e, e_gt, J + j - 3)
                    nc.scalar.activation(G[s % 4], bS[s % 2][:, :], ACT.Gelu_apprx_tanh).then_inc(e_g, 1)
                if tile_at(j - 1):
                    t = (s - 1) % RING
                    e.wait_ge(e_gt, J + j)
                    wait(e, e_y, J + j - 4)
                    nc.scalar.activation(GT[t % 4], bT[t % 2][:, :], ACT.Copy).then_inc(e_ge, 1)
            stepped(nc.scalar, step, 1)

        def experts_pool(e, k, dst):
            def step(j, s):
                wait_here(e, e_o, k * SLOTS + j + 1)
                nc.gpsimd.indirect_dma_start(
                    dst, bass.IndirectOffsetOnAxis(ap=out_tok[s % 4][:, :], axis=0), OUT[s % 4], None,
                    bounds_check=N - 1, oob_is_err=False).then_inc(e_sc[s % 4], 16)
            stepped(nc.gpsimd, step, 0)
            for s in range(4):
                e.wait_ge(e_sc[s], 16 * (SLOTS // 4) * (k + 1))

        def attention(e, body, middle=None):
            for b in range(1):
                for s in range(2):
                    body(b, s, s, True)
                with e.Fori(1, PAIRS // 2) as k:
                    for s in range(2):
                        body(b, k * 2 + s, s, False)
            with e.Fori(1, B) as b:
                for s in range(2):
                    body(b, s, s, True)
                with e.Fori(1, PAIRS // 2) as k:
                    for s in range(2):
                        body(b, k * 2 + s, s, False)

        def idx(b, p):
            return b * PAIRS + p

        def pe_proj(e, n, which, par, xbatch):
            if which == "q":
                e.wait_ge(ws_ld[par], (n - par) * 8 + 16)
                e.wait_ge(xb_ld, xbatch * 16)
            o = 0 if which == "q" else 2
            W = WS[par]
            nc.tensor.matmul(bJ[:, :], W[:, o, :], xTb[:, 0, :], start=True, stop=False)
            nc.tensor.matmul(bJ[:, :], W[:, o, :], xTb[:, 1, :], start=False, stop=False)
            nc.tensor.matmul(bJ[:, :], W[:, o + 1, :], xTb[:, 0, :], start=False, stop=True)\
                .then_inc(s_pq if which == "q" else s_pk, 1)

        def pe_proj_v(pair):
            hi, lo = wvs[:, 0, ds(pair * 128, 128)], wvs[:, 1, ds(pair * 128, 128)]
            for j in range(NJ):
                o_, c = bJ[:, 128 * j:128 * j + 128], slice(128 * j, 128 * j + 128)
                nc.tensor.matmul(o_, xTb[:, 0, c], hi, start=True, stop=False)
                nc.tensor.matmul(o_, xTb[:, 0, c], lo, start=False, stop=False)
                last = nc.tensor.matmul(o_, xTb[:, 1, c], hi, start=False, stop=True)
            last.then_inc(s_pv, 1)

        def pe_scores(e, i, par, g):
            G_ = i * NG + g
            if g == 0:
                e.wait_ge(s_qt, i + 1)
                e.wait_ge(s_kt, i + 1)
            wait(e, s_exp, G_ - 2)
            h = slice(64 * (g // 3), 64 * (g // 3) + 64)
            S = bS[g % 3]
            for qt, c0, nb in SUPER[g % 3]:
                nc.tensor.matmul(S[:, c0:c0 + 128 * nb], QT[par][h, 128 * qt:128 * qt + 128], KT[par][h, 0:128 * nb],
                                 start=True, stop=False)
                last = nc.tensor.matmul(S[:, c0 + 128 * (nb - 1):c0 + 128 * nb], identb[:, :], maskb[:, :],
                                        start=False, stop=True)
            last.then_inc(s_S, 1)

        def pe_PT(e, i, g):
            G_ = i * NG + g
            e.wait_ge(s_exp, G_ + 1)
            wait(e, s_pt, G_ - 1)
            w = sum(nb for _, _, nb in SUPER[g % 3])
            for c in range(w):
                last = nc.tensor.transpose(bT[g % 2][:, 128 * c:128 * c + 128], P[g % 3][:, 128 * c:128 * c + 128], ident[:, :])
            last.then_inc(s_T, 1)

        def pe_AV(e, i, par, g):
            G_ = i * NG + g
            e.wait_ge(s_pt, G_ + 1)
            if g == 0:
                e.wait_ge(s_vr, i + 1)
                wait(e, s_norm, i)
            hh = g // 3
            for qt, c0, nb in SUPER[g % 3]:
                u = 4 * hh + qt
                for kb in range(nb):
                    last = nc.tensor.matmul(bO[:, DH * u:DH * u + DH], PT[g % 2][:, c0 + 128 * kb:c0 + 128 * kb + 128],
                                            V[par][:, kb, DH * hh:DH * hh + DH], start=(kb == 0), stop=(kb == nb - 1))
            last.then_inc(s_av, 1)

        def pe_OT(e, i, par):
            e.wait_ge(s_norm, i + 1)
            e.wait_ge(s_vr, i + 2)
            for j in range(NJ):
                last = nc.tensor.transpose(bJ[:, 128 * j:128 * j + 128], O[par][:, j, :, :].rearrange("p h d -> p (h d)"), ident[:, :])
            last.then_inc(s_ot, 1)

        def pe_Wo(e, i, pair, batch, final):
            e.wait_ge(s_ote, i + 1)
            first_ = isinstance(pair, int) and pair == 0
            if first_:
                wait(e, s_x2, batch)
            for j in range(NJ):
                last = nc.tensor.matmul(bY[:, 128 * j:128 * j + 128], OT[:, 128 * j:128 * j + 128],
                                        wos[:, ds(pair, 1), :].rearrange("p o d -> p (o d)"),
                                        start=(first_ and j == 0), stop=final, skip_group_check=True)
            last.then_inc(s_wo, 1)

        def pe_attention(e):
            def body(b, p, s, peeled):
                i = idx(b, p)
                n = i + 1
                par, npar = s, 1 - s
                started = not (isinstance(b, int) and peeled and s == 0)
                after = peeled and not isinstance(b, int)
                pe_scores(e, i, par, 2)
                pe_PT(e, i, 0)
                if started:
                    pe_OT(e, i - 1, npar)
                pe_scores(e, i, par, 3)
                pe_PT(e, i, 1)
                pe_AV(e, i, par, 0)
                if started:
                    if s == 0:
                        if after:
                            pe_Wo(e, i - 1, PAIRS - 1, b, True)
                        else:
                            pe_Wo(e, i - 1, p - 1, b, False)
                    else:
                        pe_Wo(e, i - 1, 0 if peeled else p - 1, b, False)
                if after and s == 1:
                    pe_rank(e, b + 7, bJ)
                    e.wait_ge(r_pos, b + 8)
                pe_proj(e, n, "q", npar, (b + (p + 1) // PAIRS) + 1)
                pe_scores(e, i, par, 4)
                pe_PT(e, i, 2)
                pe_AV(e, i, par, 1)
                e.wait_ge(s_qr, n + 1)
                pe_proj(e, n, "k", npar, None)
                pe_scores(e, i, par, 5)
                pe_PT(e, i, 3)
                pe_AV(e, i, par, 2)
                e.wait_ge(s_kr, n + 1)
                if after and s == 0:
                    e.wait_ge(r_xn, 8 + 8 + b)
                    pe_norm_T(0, bJ, r_t)
                pe_scores(e, n, npar, 0)
                pe_PT(e, i, 4)
                pe_AV(e, i, par, 3)
                if after and s == 0:
                    pe_logits(e, b + 7, bJ)
                    e.wait_ge(r_oh, b + 8)
                pe_scores(e, n, npar, 1)
                pe_PT(e, i, 5)
                pe_AV(e, i, par, 4)
                pe_proj_v((p + 1) % PAIRS)
                pe_AV(e, i, par, 5)
            pe_proj(e, 0, "q", 0, 1)
            e.wait_ge(s_qr, 1)
            pe_proj(e, 0, "k", 0, None)
            e.wait_ge(s_kr, 1)
            pe_proj_v(0)
            pe_scores(e, 0, 0, 0)
            pe_scores(e, 0, 0, 1)
            attention(nc.tensor, body)
            i = B * PAIRS - 1
            pe_OT(e, i, 1)
            pe_Wo(e, i, PAIRS - 1, B, True)
            e.wait_ge(r_xn, 8 + 8 + B)
            e.wait_ge(s_ote, i + 1)
            pe_norm_T(0, bJ, r_t)
            pe_logits(e, B + 7, bJ)
            e.wait_ge(r_oh, B + 8)
            pe_rank(e, B + 7, bJ)

        def dve_max(e, i, par, g):
            e.wait_ge(s_S, i * NG + g + 1)
            for qt, c0, nb in SUPER[g % 3]:
                u = 4 * (g // 3) + qt
                last = nc.vector.tensor_reduce(nmax[par][:, u:u + 1], bS[g % 3][:, c0:c0 + 128 * nb], AX.X, ALU.max, negate=True)
            last.then_inc(s_max, 1)

        swap = [c ^ 1 for c in range(32)]

        def dve_rope(e, n, which):
            done, free, read, parts = (s_pq, s_qt, s_qr, s_qv) if which == "q" else (s_pk, s_kt, s_kr, s_kv)
            C_, S_, o = (cosq, sinq, 0) if which == "q" else (cosk, sink, 2)
            e.wait_ge(done, n + 1)
            wait(e, free, n)
            nc.vector.tensor_tensor(C_[:, :], bJ[:, :], rope[:, o, :], ALU.mult)
            nc.vector.stream_shuffle(S_[:, :], bJ[:, :], mask=swap).then_inc(read, 1)
            e.wait_ge(read, n + 1)
            nc.vector.tensor_tensor(S_[:, :], S_[:, :], rope[:, o + 1, :], ALU.mult).then_inc(parts, 1)

        def dve_x2(e, b1_):
            e.wait_ge(s_wo, b1_ * PAIRS)
            e.wait_ge(s_bo, b1_)
            x_ = PL[0][:, :, XX:XX + D]
            nc.vector.tensor_tensor(x_, bY[:, :].rearrange("p (j d) -> p j d", j=NJ), x_, ALU.add).then_inc(s_x2, 1)
            nc.vector.drain()
            dve_norm(e, 15 + b1_, 0)

        def dve_attention(e):
            def norm(i, par):
                e.wait_ge(s_av, i * NG + NG)
                nc.vector.reciprocal(rinv[:, :], rsum[par][:, :])
                nc.vector.drain()
                nc.vector.tensor_tensor(O[par][:, :, :, :].rearrange("p j h d -> p h j d"),
                                        bO[:, :].rearrange("p (h j d) -> p h j d", h=2, j=NJ),
                                        rinv[:, :].rearrange("p (h j) -> p h j", h=2).unsqueeze(3).broadcast_to([128, 2, NJ, DH]),
                                        ALU.mult).then_inc(s_norm, 1)
            def body(b, p, s, peeled):
                i = idx(b, p)
                n = i + 1
                par, npar = s, 1 - s
                after = peeled and not isinstance(b, int)
                if after and s == 1:
                    dve_max(e, i, par, 2)
                    dve_max(e, i, par, 3)
                    dve_position(e, b + 7, b - 1, 0, bJ)
                else:
                    dve_max(e, i, par, 2)
                    dve_max(e, i, par, 3)
                dve_rope(e, n, "q")
                dve_max(e, i, par, 4)
                dve_rope(e, n, "k")
                if after and s == 0:
                    dve_x2(e, b)
                dve_max(e, i, par, 5)
                dve_max(e, n, npar, 0)
                if after and s == 0:
                    dve_route(e, b + 7, bJ)
                dve_max(e, n, npar, 1)
                norm(i, par)
            dve_rope(e, 0, "q")
            dve_rope(e, 0, "k")
            dve_max(e, 0, 0, 0)
            dve_max(e, 0, 0, 1)
            attention(nc.vector, body)
            dve_x2(e, B)
            dve_route(e, B + 7, bJ)
            dve_position(e, B + 7, B - 1, 0, bJ)

        def act_attention(e):
            def exps(i, par, g):
                G_ = i * NG + g
                e.wait_ge(s_max, G_ + 1)
                wait(e, s_T, G_ - 2)
                for qt, c0, nb in SUPER[g % 3]:
                    u = 4 * (g // 3) + qt
                    last = nc.scalar.activation(P[g % 3][:, c0:c0 + 128 * nb], bS[g % 3][:, c0:c0 + 128 * nb], ACT.Exp,
                                                bias=nmax[par][:, u:u + 1], accum_out=rsum[par][:, u:u + 1])
                last.then_inc(s_exp, 1)
            def pt_out(i, g):
                G_ = i * NG + g
                e.wait_ge(s_T, G_ + 1)
                wait(e, s_av, G_ - 1)
                w = 128 * sum(nb for _, _, nb in SUPER[g % 3])
                nc.scalar.activation(PT[g % 2][:, 0:w], bT[g % 2][:, 0:w], ACT.Copy).then_inc(s_pt, 1)
            def v_out(n, par):
                e.wait_ge(s_pv, n + 1)
                wait(e, s_av, (n - 1) * NG)
                nc.scalar.activation(V[par][:, :, :], bJ[:, :].rearrange("p (j d) -> p j d", j=NJ), ACT.Copy).then_inc(s_vr, 1)
            def ot_out(i):
                e.wait_ge(s_ot, i + 1)
                wait(e, s_wo, i)
                nc.scalar.activation(OT[:, :], bJ[:, :], ACT.Copy).then_inc(s_ote, 1)
            def body(b, p, s, peeled):
                i = idx(b, p)
                n = i + 1
                par, npar = s, 1 - s
                started = not (isinstance(b, int) and peeled and s == 0)
                after = peeled and not isinstance(b, int)
                exps(i, par, 1)
                pt_out(i, 0)
                if started:
                    ot_out(i - 1)
                for g in range(1, NG):
                    if g < NG - 1:
                        exps(i, par, g + 1)
                    else:
                        exps(n, npar, 0)
                    pt_out(i, g)
                    if after and s == 0 and g == 3:
                        act_xT(e, b + 7, bJ)
                    if after and s == 1 and g == 1:
                        act_exp(e, b + 7)
                v_out(n, npar)
            v_out(0, 0)
            exps(0, 0, 0)
            attention(nc.scalar, body)
            ot_out(B * PAIRS - 1)
            act_xT(e, B + 7, bJ)
            act_exp(e, B + 7)

        def pool_attention(e):
            def add(n, par, which):
                parts, done, dst, C_, S_ = (s_qv, s_qt, QT, cosq, sinq) if which == "q" else (s_kv, s_kt, KT, cosk, sink)
                e.wait_ge(parts, n + 1)
                wait(e, s_S, (n - 1) * NG)
                nc.gpsimd.tensor_tensor(dst[par][:, :], C_[:, :], S_[:, :], ALU.add).then_inc(done, 1)
            def body(b, p, s, peeled):
                i = idx(b, p)
                add(i + 1, 1 - s, "q")
                add(i + 1, 1 - s, "k")
                if peeled and s == 0 and not isinstance(b, int):
                    pool_rstd(e, b + 15)
                if peeled and s == 1:
                    if not isinstance(b, int):
                        pool_scatter(e, b + 7, 0)
                    e.wait_ge(x_ld[0], 16 * (8 + 1) + b * 16)
                    for j in range(NJ):
                        last = nc.gpsimd.tensor_tensor(PL[0][:, j, XX:XX + D], PL[0][:, j, XX:XX + D], bo_bc[:, :], ALU.add)
                    last.then_inc(s_bo, 1)
            add(0, 0, "q")
            add(0, 0, "k")
            attention(nc.gpsimd, body)
            pool_rstd(e, B + 15)
            pool_scatter(e, B + 7, 0)

        def sp_attention(e):
            def load_w(n, par, pair):
                wait_here(e, s_pk, n - 1)
                e.dma_start(WS[par][:, :, :].bitcast(f32), wqk[:, :, ds(pair * 128, 128)].bitcast(f32)).then_inc(ws_ld[par], 16)
            def load_x(b):
                e.dma_start(xTb[:, :, :].bitcast(f32), xnT[:, :, ds(b * T, T)].bitcast(f32)).then_inc(xb_ld, 16)
            e.wait_ge(l_hi, B)
            e.wait_ge(l_lo, B)
            load_w(0, 0, 0)
            load_w(1, 1, 1)
            load_x(0)
            def payload(b):
                wait_here(e, r_sc[0], 64 * 4 + b * 64)
                e.dma_start(PL[0][:, :, XX:XX + D], xrows(x1, b)).then_inc(x_ld[0], 16)
            def batch(b):
                for s in range(2):
                    load_w(idx(b, s + 2), s, s + 2)
                payload(b)
                with nc.sync.Fori(1, PAIRS // 2 - 1) as k:
                    for s in range(2):
                        load_w(idx(b, k * 2 + s + 2), s, k * 2 + s + 2)
                for s in range(2):
                    load_w(idx(b, PAIRS + s), s, s)
                wait_here(e, s_pv, b * PAIRS + PAIRS)
            batch(0)
            with nc.sync.Fori(1, B) as b:
                load_x(b)
                batch(b)
            load_x(0)

        block = ctx.enter_context(nc.Block())

        @block.sync
        def _(sp):
            for dst, src in ((ident, c_ident), (rope, c_rope), (small, c_small)):
                sp.dma_start(dst[:], src).then_inc(c_ld, 16)
            sp.dma_start(slot_c[:, :], c_slots).then_inc(c_ld, 16)
            sp.dma_start(swt[:, :], sw).then_inc(c_ld, 16)
            sp.dma_start(bo_bc[:, :], bo.rearrange("(o d) -> o d", o=1).broadcast_to([128, D])).then_inc(c_ld, 16)
            sp.dma_start(sbias[:, :, :], sb_.rearrange("(o j e) -> o j e", o=1, j=1).broadcast_to([128, NJ, EX])).then_inc(c_ld, 16)
            for b in range(B):
                par = b % 2
                if b >= 2:
                    sp.wait_ge(r_sc[par], 64 * (b // 2))
                sp.dma_start(PL[par][:, :, XX:XX + D], xrows(x, b)).then_inc(x_ld[par], 16)
            sp.wait_ge(prep, 1)
            for s_ in range(SPARE):
                r0 = EX * REGION + s_ * TILE
                sp.dma_start(region[r0:r0 + TILE, :], pad[:, :]).then_inc(spare_st, 16)
            sp_pads(sp, 0, [256, 256])
            experts_sp(sp, 0)
            all_meet(sp, 1)
            for b in range(B):
                par = b % 2
                if b >= 2:
                    sp.wait_ge(l_t, b - 1)
                sp.dma_start(PL[par][:, :, XX:XX + D], xrows(x1, b)).then_inc(x_ld[par], 16)
            sp_attention(sp)
            sp_pads(sp, 1, [64 * 4 + 64 * B, 256])
            all_meet(sp, 2)
            experts_sp(sp, 1)
            all_meet(sp, 3)

        @block.scalar
        def _(act):
            act.dma_start(bias_raw[:, 0:32], b1.rearrange("e (a c) -> (e a) c", c=32)).then_inc(w2_ld, 16)
            act.dma_start(bias_raw[:, 32:40], b2.rearrange("e (a c) -> (e a) c", c=8)).then_inc(w2_ld, 16)
            act.dma_start(w2s[:, :, :, :], w2.rearrange("e (c p) d -> p e c d", p=128)).then_inc(w2_ld, 16)
            act.dma_start(wos[:, :, :], wo.rearrange("(a p) d -> p a d", p=128)).then_inc(w2_ld, 16)
            for c in range(2):
                act.dma_start(raw[c][:, :], chunks[c][0]).then_inc(raw_ld[c], 16)
            def high(c):
                act.wait_ge(raw_ld[c % 2], 16 * (c // 2 + 1))
                nc.scalar.activation(chunks[c][1], raw[c % 2][:, :], ACT.Copy).then_inc(raw_hi, 1)
                if c + 1 >= 2 and c + 1 < NCH:
                    act.wait_ge(raw_lo, c)
                    act.dma_start(raw[(c + 1) % 2][:, :], chunks[c + 1][0]).then_inc(raw_ld[(c + 1) % 2], 16)
            act.wait_ge(w2_ld, 64)
            nc.scalar.activation(bias_hl[:, 0, :], bias_raw[:, :], ACT.Copy).then_inc(bias_hi, 1)
            high(0)
            for b in range(B):
                act_xT(act, b, bJ)
                act_exp(act, b)
                if b < NCH - 1:
                    high(b + 1)
            for c in range(B + 1, NCH):
                high(c)
            experts_act(act, 0)
            all_meet(act, 1)
            for b in range(B):
                act.wait_ge(l_t, b + 1)
                nc.scalar.activation(xnT[:, 0, b * T:(b + 1) * T], bT[b % 2][:, :], ACT.Copy).then_inc(l_hi, 1)
            act_attention(act)
            all_meet(act, 2)
            experts_act(act, 1)
            all_meet(act, 3)

        @block.gpsimd
        def _(pool):
            nc.gpsimd.memset(pad[:, :], 0.0)
            pool.drain()
            nc.gpsimd.memset(pad[:, TOK:TOK + 1].bitcast(i32), NOWHERE)
            nc.gpsimd.iota(tokens[:, :], [[TILE, N // TILE]], base=0, channel_multiplier=1)
            nc.gpsimd.memset(onesb[:, :], 1.0)
            nc.gpsimd.memset(mhalf[:, :], -0.5)
            nc.gpsimd.memset(onesr[:, :].bitcast(f32), 1.0)
            nc.gpsimd.dma_start(identb[:, :], c_ident).then_inc(bias_ld, 16)
            nc.gpsimd.dma_start(maskb[:, :], c_mask).then_inc(bias_ld, 16)
            nc.gpsimd.dma_start(upperb[:, :], c_upper).then_inc(bias_ld, 16)
            pool.drain().then_inc(prep, 1)
            pool.wait_ge(bias_hi, 1)
            nc.gpsimd.tensor_tensor(bias_hl[:, 1, :], bias_raw[:, :], bias_hl[:, 0, :], ALU.subtract)
            pool.drain()
            for r in range(2):
                nc.gpsimd.dma_start(b1s[r:r + 1, :].rearrange("o (a c) -> o a c", c=32).bitcast(f32), bias_hl[:, r, 0:32].bitcast(f32)).then_inc(bias_ld, 16)
                nc.gpsimd.dma_start(b2s[r:r + 1, :].rearrange("o (a c) -> o a c", c=8).bitcast(f32), bias_hl[:, r, 32:40].bitcast(f32)).then_inc(bias_ld, 16)
            def low(c):
                pool.wait_ge(raw_hi, c + 1)
                nc.gpsimd.tensor_tensor(chunks[c][2], raw[c % 2][:, :], chunks[c][1], ALU.subtract).then_inc(raw_lo, 1)
            pool_rstd(pool, 0)
            for b in range(B):
                if b + 1 < B:
                    pool_rstd(pool, b + 1)
                low(b)
                pool_scatter(pool, b, b % 2)
            for c in range(B, NCH):
                low(c)
            experts_pool(pool, 0, x1)
            all_meet(pool, 1)
            for b in range(B):
                pool_rstd(pool, B + b)
            pool_attention(pool)
            all_meet(pool, 2)
            experts_pool(pool, 1, out)
            all_meet(pool, 3)

        @block.vector
        def _(dve):
            nc.vector.memset(cum[:, :], 0.0)
            dve.wait_ge(c_ld, 112)
            dve.wait_ge(prep, 1)
            dve.wait_ge(x_ld[0], 16)
            dve_norm(dve, 0, 0)
            for b in range(B):
                if b + 1 < B:
                    dve.wait_ge(x_ld[(b + 1) % 2], 16 * ((b + 1) // 2 + 1))
                    dve_norm(dve, b + 1, (b + 1) % 2)
                dve_route(dve, b, bY)
                dve_position(dve, b, b, b % 2, bO)
            dve.drain()
            dve_table(dve, 0)
            experts_dve(dve, 0)
            all_meet(dve, 1)
            nc.vector.memset(cum[:, :], 0.0)
            for b in range(B):
                dve.wait_ge(x_ld[b % 2], 16 * (4 + b // 2 + 1))
                dve_norm(dve, B + b, b % 2)
                dve.wait_ge(l_hi, b + 1)
                nc.vector.tensor_tensor(xnT[:, 1, b * T:(b + 1) * T], bT[b % 2][:, :], xnT[:, 0, b * T:(b + 1) * T],
                                        ALU.subtract).then_inc(l_lo, 1)
            dve_attention(dve)
            dve.drain()
            dve_table(dve, 1)
            all_meet(dve, 2)
            experts_dve(dve, 1)
            all_meet(dve, 3)

        @block.tensor
        def _(pe):
            pe.wait_ge(c_ld, 112)
            pe.wait_ge(bias_ld, 112)
            pe.wait_ge(prep, 1)
            for b in range(B):
                pe.wait_ge(r_xn, b + 1)
                wait(pe, r_xt, b)
                pe_norm_T(b % 2, bJ, r_t)
                pe_logits(pe, b, bY)
                pe_rank(pe, b, bO)
            pe_counts(pe, 0)
            pe.wait_ge(r_tab, 1)
            pe.wait_ge(raw_lo, EX)
            pe.wait_ge(w2_ld, 64)
            experts_pe(pe, 0)
            all_meet(pe, 1)
            for b in range(B):
                pe.wait_ge(r_xn, B + b + 1)
                wait(pe, l_lo, b - 1)
                pe_norm_T(b % 2, bT[b % 2], l_t)
            pe.wait_ge(l_lo, B)
            pe.wait_ge(raw_lo, NCH)
            pe_attention(pe)
            pe_counts(pe, 1)
            all_meet(pe, 2)
            experts_pe(pe, 1)
            all_meet(pe, 3)


_INS = ["L0_attn_x", "L0_attn_Wq", "L0_attn_Wk", "L0_attn_Wv", "L0_attn_Wo", "L0_attn_bo",
        "L0_ffn_switch_w", "L0_ffn_switch_b", "L0_ffn_w1", "L0_ffn_b1", "L0_ffn_w2", "L0_ffn_b2"]


def _constants():
    f = np.float32
    p = np.arange(128)
    inv = (1.0 / 10000.0 ** (np.arange(0, DH, 2, dtype=f) / f(DH))).astype(f)
    ang = (np.arange(T, dtype=f)[:, None] * inv[None, :]).astype(f)
    cos = np.cos(ang).astype(f)[:, (p % DH) // 2].T
    sin = np.sin(ang).astype(f)[:, (p % DH) // 2].T * np.where(p % 2 == 0, -1, 1)[:, None].astype(f)
    scale = f(DH ** -0.5)
    rope = np.stack([cos * scale, sin * scale, cos, sin], 1).astype(f)
    e = np.arange(EX, dtype=f)
    small = np.zeros((128, 2, NJ, EX), f)
    small[:, 0], small[:, 1] = EX - e, e * REGION
    s = np.arange(SLOTS, dtype=f)
    slots = np.concatenate([s * TILE, np.repeat(s, EX), (e[None, :] <= e[:, None]).astype(f).ravel(),
                            np.tile(np.arange(32, dtype=f) * TILE, EX)])[None]
    return {
        "ident": np.eye(128, dtype=f),
        "mask": np.where(p[None, :] > p[:, None], MASKED, 0).astype(f),
        "upper": (p[:, None] < p[None, :]).astype(f),
        "rope": rope, "small": small, "slots": slots.astype(f),
    }


def kernel(**inputs):
    import concourse.bacc as _bacc
    from concourse.bass_utils import run_bass_kernel_spmd as _run

    nc = _bacc.Bacc("TRN2", target_bir_lowering=False, num_devices=1)
    arrays, args = {}, []

    def given(name, a):
        a = np.ascontiguousarray(a)
        arrays[name] = a
        args.append(nc.dram_tensor(name, a.shape, mybir.dt.from_np(a.dtype), kind="ExternalInput").ap())

    for name in _INS:
        a = np.asarray(inputs[name])
        if name == "L0_attn_x":
            a = a.reshape(N, D)
        given(f"in_{name}", a)
    for name, a in _constants().items():
        given(f"const_{name}", a)
    out = nc.dram_tensor("out_0", (N, D), mybir.dt.float32, kind="ExternalOutput").ap()
    macaron_kernel(nc, *args, out)
    r = _run(nc, [arrays], core_ids=[0])
    return np.asarray(r.results[0]["out_0"]).reshape(B, T, D)
```

```python
from contextlib import ExitStack

import numpy as np

import concourse.bass as bass
from concourse import mybir

B, T, D = 8, 512, 128
TILE = 128
NJ = T // TILE
N = B * T
HEADS, DH = 16, 64
PAIRS = HEADS // 2
EX, F = 8, 512
FC = F // 128
RING = 8
SLOTS = -(-(N // TILE + EX - 1) // RING) * RING
REGION = N + TILE
SPARE = SLOTS - N // TILE
ROWS = EX * REGION + SPARE * TILE
XN, XX, GATE, TOK, ROW = 0, D, 2 * D, 2 * D + 1, 2 * D + 2
NOWHERE = 1 << 20
NPL = 4
EPS = 1e-5
MASKED = -1e30
SUPER = [[(3, 0, 4)], [(0, 0, 1), (2, 128, 3)], [(1, 0, 2)]]
NG = 2 * len(SUPER)


def macaron_kernel(nc, x, wq, wk, wv, wo, bo, sw, sb_, w1, b1, w2, b2,
                   c_ident, c_mask, c_upper, c_rope, c_small, c_slots, out):
    f32, f32r, bf16, i32 = mybir.dt.float32, mybir.dt.float32r, mybir.dt.bfloat16, mybir.dt.int32
    ALU, ACT, AX = mybir.AluOpType, mybir.ActivationFunctionType, mybir.AxisListType
    ds = bass.ds
    ctx = ExitStack()
    with ctx:
        def sb(name, shape, dt=f32):
            return ctx.enter_context(nc.sbuf_tensor(name, shape, dt))

        def sem(name):
            return ctx.enter_context(nc.semaphore(name))

        region = nc.dram_tensor("routed_rows", [ROWS, ROW], f32).ap()
        x1 = nc.dram_tensor("x_after_ffn1", [N, D], f32).ap()

        ident = sb("ident", [128, 128])
        identb = sb("identb", [128, 128], bf16)
        maskb = sb("maskb", [128, 128], bf16)
        upperb = sb("upperb", [128, 128], bf16)
        onesb = sb("onesb", [128, 128], bf16)
        onesr = sb("onesr", [2, 128], f32r)
        rope = sb("rope", [128, 4, T])
        small = sb("small", [128, 2, NJ, EX])
        sbias = sb("sbias", [128, NJ, EX])
        slot_c = sb("slot_c", [1, SLOTS + SLOTS * EX + EX * EX + EX * 32])
        tokens = sb("tokens", [128, N // TILE], i32)
        bo_bc = sb("bo_bc", [128, D])
        swt = sb("swt", [128, EX])
        w1s = sb("w1s", [128, 2, EX * F], f32r)
        w2s = sb("w2s", [128, EX, FC, D])
        b1s = sb("b1s", [2, EX * F], f32r)
        b2s = sb("b2s", [2, EX * D], f32r)
        wqk = sb("wqk", [128, 4, HEADS * DH], f32r)
        wvs = sb("wvs", [128, 2, HEADS * DH], f32r)
        wos = sb("wos", [128, PAIRS, D])

        raw = [sb(f"raw{i}", [128, 512]) for i in range(2)]
        bias_hl = sb("bias_hl", [128, 2, 40], f32r)
        bias_raw = sb("bias_raw", [128, 40])
        PL = [sb(f"payload{i}", [128, NJ, ROW]) for i in range(NPL)]
        pad = sb("pad", [128, ROW])
        stats = sb("stats", [128, NJ, 6])
        mv = sb("mv", [128, NJ, 2])
        var = sb("var", [128, NJ])
        rstd = sb("rstd", [128, NJ])
        mhalf = sb("mhalf", [128, NJ])
        xT = sb("xT", [128, T])
        lg = sb("lg", [128, NJ, EX])
        lmax = sb("lmax", [128, NJ])
        ldiff = sb("ldiff", [128, NJ, EX])
        lexp = sb("lexp", [128, NJ, EX])
        lsum = sb("lsum", [128, NJ])
        eq = sb("eq", [128, NJ, EX])
        first = sb("first", [128, NJ])
        oh = sb("oh", [128, NJ, EX])
        ohb = sb("ohb", [128, NJ, EX], bf16)
        ohsum = sb("ohsum", [128, EX])
        cum = sb("cum", [128, EX])
        cumb = sb("cumb", [128, EX], bf16)
        rk = sb("rk", [128, NJ, EX])
        posf = sb("posf", [128, NJ])
        pos = [sb(f"pos{i}", [128, NJ], i32) for i in range(NPL)]
        cnt = sb("cnt", [1, EX])
        tiles_e = sb("tiles_e", [1, EX])
        tri = sb("tri", [1, EX, EX])
        ends = sb("ends", [1, EX])
        skip = sb("skip", [1, EX])
        sl_e = sb("sl_e", [1, SLOTS])
        sl_r = sb("sl_r", [1, SLOTS])
        slot_expert = sb("slot_expert", [1, SLOTS], i32)
        slot_row = sb("slot_row", [1, SLOTS], i32)
        pad_row = sb("pad_row", [1, EX], i32)
        QT = [sb(f"qT{i}", [128, T]) for i in range(2)]
        KT = [sb(f"kT{i}", [128, T]) for i in range(2)]
        cosq, sinq, cosk, sink = [sb(n, [128, T]) for n in ("x_cosq", "x_sinq", "x_cosk", "x_sink")]
        P = [sb(f"P{i}", [128, 512]) for i in range(3)]
        ge, ge2 = [P[i][0:1, 0:SLOTS * EX].rearrange("p (s e) -> p s e", e=EX) for i in range(2)]
        cmp32 = P[2][0:1, 0:EX * 32].rearrange("p (e s) -> p e s", s=32)
        PT = [sb(f"PT{i}", [128, 512]) for i in range(2)]
        V = [sb(f"V{i}", [128, NJ, 128]) for i in range(2)]
        O = [sb(f"O{i}", [128, NJ, 2, DH]) for i in range(2)]
        OT = sb("OT", [128, T])
        WS = [sb(f"WS{i}", [128, 4, 128], f32r) for i in range(2)]
        xTb = sb("xTb", [128, 2, T], f32r)
        xTn = sb("xTn", [128, 2, T], f32r)
        nmax = [sb(f"nmax{i}", [128, 8]) for i in range(2)]
        rsum = [sb(f"rsum{i}", [128, 8]) for i in range(2)]
        rinv = sb("rinv", [128, 8])
        flatV = [t[:, :, :].rearrange("p j d -> p (j d)") for t in V]
        flatO = [t[:, :, :, :].rearrange("p j h d -> p (j h d)") for t in O]
        XS = [t[:, 0:ROW] for t in (*QT, *KT, sinq, cosk, *flatV)]
        XH = [sb(f"xh{i}", [128, 128], f32r) for i in range(2)]
        XL = [sb(f"xl{i}", [128, 128], f32r) for i in range(2)]
        G = [P[0][:, :], P[1][:, :], P[2][:, :], flatO[0]]
        GT = [PT[0][:, :], PT[1][:, :], cosq[:, :], sink[:, :]]
        OUT = [OT[:, 128 * i:128 * i + 128] for i in range(4)]
        out_tok = [sb(f"out_tok{i}", [128, 1], i32) for i in range(4)]

        bank = [ctx.enter_context(nc.psum_tensor(f"bank{i}", [128, 512], f32)) for i in range(8)]
        bS, bT, bJ, bO, bY = bank[0:3], bank[3:5], bank[5], bank[6], bank[7]

        c_ld, c_ld2, raw_ld0, raw_ld1, raw_hi, raw_lo = [sem(n) for n in (
            "consts_loaded", "late_consts_loaded", "raw_loaded0", "raw_loaded1", "raw_high", "raw_low")]
        raw_ld = [raw_ld0, raw_ld1]
        prep, bias_hi, bias_lo, bias_ld, w2_ld = [sem(n) for n in (
            "prep", "bias_high", "bias_low", "bias_rows", "w2_loaded")]
        spare_st = sem("spare_rows_stored")
        x_ld = [sem(f"x_loaded{i}") for i in range(NPL)]
        r_sc = [sem(f"rows_scattered{i}") for i in range(NPL)]
        r_var, r_rstd, r_xn, r_t, r_xt, r_lg, r_d, r_ex, r_oh, r_rk, r_rkr, r_pos, r_cnt, r_tab, r_pad = [sem("router_" + n) for n in (
            "var", "rstd", "normed", "transposed", "xT", "logits", "diff", "exp", "onehot", "rank", "rank_read", "pos", "counts", "table", "padded")]
        e_ld = [sem(f"tile_loaded{i}") for i in range(RING)]
        e_sc = [sem(f"tile_scattered{i}") for i in range(4)]
        e_tx, e_xs, e_h, e_g, e_gt, e_ge, e_y, e_o = [sem("expert_" + n) for n in (
            "xT", "xsplit", "hidden", "gelu", "hiddenT", "hiddenT_out", "y", "out")]
        l_var, l_rstd, l_xn, l_t, l_hi, l_lo = [sem("ln_" + n) for n in (
            "var", "rstd", "normed", "transposed", "high", "low")]
        ws_ld = [sem("ws_loaded0"), sem("ws_loaded1")]
        xb_ld, tick, phase = sem("xTb_loaded"), sem("tick"), sem("phase")
        s_pq, s_pk, s_pv, s_qr, s_kr, s_vr, s_qv, s_kv, s_qt, s_kt = [sem("a_" + n) for n in (
            "proj_q", "proj_k", "proj_v", "q_read", "k_read", "v_read", "q_parts", "k_parts", "q_roped", "k_roped")]
        s_S, s_max, s_exp, s_T, s_pt, s_av, s_norm, s_ot, s_ote, s_wo, s_x2, s_bo = [sem("a_" + n) for n in (
            "scores", "max", "exp", "PT", "PT_out", "AV", "norm", "OT", "OT_out", "wo", "x2", "bo")]

        def wait(e, s, v):
            if not isinstance(v, int) or v > 0:
                e.wait_ge(s, v)

        def wait_here(e, s, v):
            wait(e, s, v)
            e.sem_inc(tick, 1)

        def all_meet(e, k):
            e.drain().then_inc(phase, 1)
            e.wait_ge(phase, 5 * k)

        chunks = [(w1[e], w1s[:, 0, e * F:(e + 1) * F], w1s[:, 1, e * F:(e + 1) * F]) for e in range(EX)]
        for w, dst, k in ((wq, wqk, 0), (wk, wqk, 2), (wv, wvs, 0)):
            for h in range(2):
                cols = slice(512 * h, 512 * h + 512)
                chunks.append((w[:, cols], dst[:, k, cols], dst[:, k + 1, cols]))
        NCH = len(chunks)

        def xrows(src, b):
            return src.rearrange("(b j p) d -> b p j d", p=TILE, j=NJ)[ds(b, 1)].rearrange("o p j d -> p (o j) d")

        for_router, for_attention = (r_var, r_rstd, r_xn), (l_var, l_rstd, l_xn)

        def pool_rstd(e, m, use):
            e.wait_ge(use[0], m + 1)
            nc.gpsimd.tensor_tensor(rstd[:, :], var[:, :], mhalf[:, :], ALU.pow).then_inc(use[1], 1)

        def dve_stats(par, use):
            for j in range(NJ):
                nc.vector.bn_stats(stats[:, j, :], PL[par][:, j, XX:XX + D])
            nc.vector.drain()
            for j in range(NJ):
                nc.vector.bn_aggr(mv[:, j, :], stats[:, j, :])
            nc.vector.drain()
            nc.vector.tensor_scalar(var[:, :], mv[:, :, 1], EPS, None, ALU.add).then_inc(use[0], 1)

        def dve_norm(e, m, par, use):
            e.wait_ge(use[1], m + 1)
            for j in range(NJ):
                last = nc.vector.tensor_scalar(PL[par][:, j, XN:XN + D], PL[par][:, j, XX:XX + D],
                                               mv[:, j, 0:1], rstd[:, j:j + 1], ALU.subtract, ALU.mult)
            last.then_inc(use[2], 1)

        def pe_norm_T(par, bankT, done):
            for j in range(NJ):
                last = nc.tensor.transpose(bankT[:, 128 * j:128 * j + 128], PL[par][:, j, XN:XN + D], ident[:, :])
            last.then_inc(done, 1)

        def act_xT(e, n, bankT):
            e.wait_ge(r_t, n + 1)
            wait(e, r_lg, n)
            nc.scalar.activation(xT[:, :], bankT[:, :], ACT.Copy).then_inc(r_xt, 1)

        def pe_logits(e, n, bankL):
            e.wait_ge(r_xt, n + 1)
            for j in range(NJ):
                last = nc.tensor.matmul(bankL[:, EX * j:EX * j + EX], xT[:, 128 * j:128 * j + 128], swt[:, :],
                                        start=True, stop=True)
            last.then_inc(r_lg, 1)

        def dve_route(e, n, bankL):
            V_ = nc.vector
            e.wait_ge(r_lg, n + 1)
            V_.tensor_tensor(lg[:, :, :], bankL[:, 0:NJ * EX].rearrange("p (j e) -> p j e", j=NJ), sbias[:, :, :], ALU.add)
            V_.drain()
            V_.tensor_reduce(lmax[:, :], lg[:, :, :], AX.X, ALU.max)
            V_.drain()
            top = lmax[:, :].unsqueeze(2).broadcast_to([128, NJ, EX])
            V_.tensor_tensor(ldiff[:, :, :], lg[:, :, :], top, ALU.subtract).then_inc(r_d, 1)
            V_.tensor_tensor(eq[:, :, :], lg[:, :, :], top, ALU.is_equal)
            V_.drain()
            V_.tensor_tensor(eq[:, :, :], eq[:, :, :], small[:, 0], ALU.mult)
            V_.drain()
            V_.tensor_reduce(first[:, :], eq[:, :, :], AX.X, ALU.max)
            V_.drain()
            V_.tensor_tensor(oh[:, :, :], small[:, 0], first[:, :].unsqueeze(2).broadcast_to([128, NJ, EX]), ALU.is_equal)
            V_.drain()
            V_.tensor_copy(ohb[:, :, :], oh[:, :, :])
            V_.tensor_copy(cumb[:, :], cum[:, :]).then_inc(r_oh, 1)

        def act_exp(e, n):
            e.wait_ge(r_d, n + 1)
            nc.scalar.activation(lexp[:, :, :], ldiff[:, :, :], ACT.Exp).then_inc(r_ex, 1)

        def pe_rank(e, n, bankR):
            e.wait_ge(r_oh, n + 1)
            R = bankR[:, 0:NJ * EX]
            nc.tensor.matmul(R, onesb[:, :], cumb[:, :].unsqueeze(1).broadcast_to([128, NJ, EX]), start=True, stop=False)
            for j in range(NJ - 1):
                nc.tensor.matmul(bankR[:, EX * (j + 1):NJ * EX], onesb[:, :],
                                 ohb[:, j:j + 1, :].broadcast_to([128, NJ - 1 - j, EX]), start=False, stop=False)
            nc.tensor.matmul(R, upperb[:, :], ohb[:, :, :], start=False, stop=True).then_inc(r_rk, 1)

        def dve_position(e, n, b, par, bankR):
            V_ = nc.vector
            e.wait_ge(r_rk, n + 1)
            V_.tensor_tensor(rk[:, :, :], bankR[:, 0:NJ * EX].rearrange("p (j e) -> p j e", j=NJ), small[:, 1], ALU.add)\
                .then_inc(r_rkr, 1)
            V_.tensor_reduce(ohsum[:, :], oh[:, :, :].rearrange("p j e -> p e j"), AX.X, ALU.add)
            V_.drain()
            V_.tensor_tensor(rk[:, :, :], rk[:, :, :], oh[:, :, :], ALU.mult)
            V_.tensor_tensor(cum[:, :], cum[:, :], ohsum[:, :], ALU.add)
            V_.drain()
            V_.tensor_reduce(posf[:, :], rk[:, :, :], AX.X, ALU.add)
            e.wait_ge(r_ex, n + 1)
            V_.tensor_reduce(lsum[:, :], lexp[:, :, :], AX.X, ALU.add)
            V_.drain()
            V_.reciprocal(lsum[:, :], lsum[:, :])
            V_.tensor_copy(PL[par][:, :, TOK:TOK + 1].bitcast(i32).rearrange("p j o -> p (j o)"), tokens[:, ds(b * NJ, NJ)])
            V_.drain()
            V_.tensor_scalar(PL[par][:, :, GATE], lsum[:, :], 0.5, None, ALU.mult)
            V_.tensor_copy(pos[par][:, :], posf[:, :]).then_inc(r_pos, 1)

        def pool_scatter(e, n, par):
            wait_here(e, r_pos, n + 1)
            for j in range(NJ):
                nc.gpsimd.indirect_dma_start(region, bass.IndirectOffsetOnAxis(ap=pos[par][:, j:j + 1], axis=0),
                                             PL[par][:, j, :], None).then_inc(r_sc[par], 16)

        def pe_counts(e, k):
            e.wait_ge(r_cnt, 2 * k + 1)
            nc.tensor.matmul(bY[:, 0:EX], onesb[:, :], cumb[:, :], start=True, stop=True).then_inc(r_cnt, 1)

        def dve_table(e, k):
            V_ = nc.vector
            o = 0
            jota = slot_c[:, o:o + SLOTS]; o += SLOTS
            jb = slot_c[:, o:o + SLOTS * EX].rearrange("p (s e) -> p s e", e=EX); o += SLOTS * EX
            low = slot_c[:, o:o + EX * EX].rearrange("p (a c) -> p a c", c=EX); o += EX * EX
            steps = slot_c[:, o:o + EX * 32].rearrange("p (e s) -> p e s", s=32)
            V_.tensor_copy(cumb[:, :], cum[:, :]).then_inc(r_cnt, 1)
            e.wait_ge(r_cnt, 2 * k + 2)
            V_.tensor_copy(cnt[:, :], bY[0:1, 0:EX])
            V_.drain()
            V_.tensor_tensor(cmp32[:, :, :], steps, cnt[:, :].unsqueeze(2).broadcast_to([1, EX, 32]), ALU.is_lt)
            V_.tensor_tensor(skip[:, :], cnt[:, :], small[0:1, 1, 0, :], ALU.add)
            V_.drain()
            V_.tensor_copy(pad_row[:, :], skip[:, :])
            V_.tensor_reduce(tiles_e[:, :], cmp32[:, :, :], AX.X, ALU.add)
            V_.drain()
            V_.tensor_tensor(tri[:, :, :], low, tiles_e[:, :].unsqueeze(1).broadcast_to([1, EX, EX]), ALU.mult)
            V_.tensor_scalar(skip[:, :], tiles_e[:, :], -float(TILE), float(REGION), ALU.mult, ALU.add)
            V_.drain()
            V_.tensor_reduce(ends[:, :], tri[:, :, :], AX.X, ALU.add)
            V_.drain()
            V_.tensor_tensor(ge[:, :, :], jb, ends[:, :].unsqueeze(1).broadcast_to([1, SLOTS, EX]), ALU.is_ge)
            V_.drain()
            V_.tensor_reduce(sl_e[:, :], ge[:, :, :], AX.X, ALU.add)
            V_.tensor_tensor(ge2[:, :, :], ge[:, :, :], skip[:, :].unsqueeze(1).broadcast_to([1, SLOTS, EX]), ALU.mult)
            V_.drain()
            V_.tensor_reduce(sl_r[:, :], ge2[:, :, :], AX.X, ALU.add)
            V_.tensor_scalar(sl_e[:, :], sl_e[:, :], float(EX - 1), None, ALU.min)
            V_.drain()
            V_.tensor_tensor(sl_r[:, :], sl_r[:, :], jota, ALU.add)
            V_.tensor_copy(slot_expert[:, :], sl_e[:, :])
            V_.drain()
            V_.tensor_copy(slot_row[:, :], sl_r[:, :]).then_inc(r_tab, 1)

        def sp_pads(e, k, scattered):
            e.wait_ge(r_tab, k + 1)
            for par in range(NPL):
                wait(e, r_sc[par], scattered[par])
            for x_ in range(EX):
                row = nc.sync.value_load(pad_row[0:1, x_:x_ + 1], min_val=0, max_val=EX * REGION - TILE)
                e.dma_start(region[ds(row, TILE), :], pad[:, :]).then_inc(r_pad, 16)

        def stepped(engine, step, lag):
            for j in range(RING):
                step(j, j)
            with engine.Fori(1, SLOTS // RING - 1) as t:
                for s in range(RING):
                    step(t * RING + s, s)
            for j in range(SLOTS - RING, SLOTS + lag):
                step(j, j % RING)

        def tile_at(j, lo=0):
            return not isinstance(j, int) or lo <= j < SLOTS

        def uses(k, j, ring):
            return j // ring + (k * (SLOTS // ring) + 1)

        def expert_of(engine, j):
            return engine.value_load(slot_expert[0:1, ds(j, 1)], min_val=0, max_val=EX - 1)

        def experts_sp(e, k):
            e.wait_ge(r_pad, 16 * EX * (k + 1))
            if k == 0:
                e.wait_ge(spare_st, 16 * SPARE)
            def step(j, s):
                wait_here(e, e_o, k * SLOTS + j - (RING - 1))
                row = nc.sync.value_load(slot_row[0:1, ds(j, 1)], min_val=0, max_val=ROWS - TILE)
                e.dma_start(XS[s], region[ds(row, TILE), :]).then_inc(e_ld[s], 16)
            stepped(nc.sync, step, 0)

        def experts_pe(e, k):
            J = k * SLOTS
            def tx(j, s):
                e.wait_ge(e_ld[s], 16 * uses(k, j, RING))
                wait(e, e_xs, J + j)
                nc.tensor.transpose(bJ[:, 0:128], XS[s][:, XN:XN + D], ident[:, :]).then_inc(e_tx, 1)
            def hidden(j, s, ex):
                e.wait_ge(e_xs, J + j + 1)
                wait(e, e_g, J + j - 1)
                s = s % 2
                hi, lo = w1s[:, 0, ds(ex * F, F)], w1s[:, 1, ds(ex * F, F)]
                nc.tensor.matmul(bS[s][:, :], XH[s][:, :], hi, start=True, stop=False)
                nc.tensor.matmul(bS[s][:, :], XH[s][:, :], lo, start=False, stop=False)
                nc.tensor.matmul(bS[s][:, :], XL[s][:, :], hi, start=False, stop=False)
                nc.tensor.matmul(bS[s][:, :], onesr[:, :], b1s[:, ds(ex * F, F)], start=False, stop=True).then_inc(e_h, 1)
            def hidden_T(j, s):
                e.wait_ge(e_g, J + j + 1)
                wait(e, e_ge, J + j - 1)
                for c in range(FC):
                    last = nc.tensor.transpose(bT[s % 2][:, 128 * c:128 * c + 128], G[s % 4][:, 128 * c:128 * c + 128],
                                               ident[:, :])
                last.then_inc(e_gt, 1)
            def down(j, s, ex):
                e.wait_ge(e_ge, J + j + 1)
                wait(e, e_o, J + j)
                for c in range(FC):
                    nc.tensor.matmul(bY[:, 0:D], GT[s % 4][:, 128 * c:128 * c + 128],
                                     w2s[:, ds(ex, 1), c, :].rearrange("p o d -> p (o d)"), start=(c == 0), stop=False)
                nc.tensor.matmul(bY[:, 0:D], onesr[:, :], b2s[:, ds(ex * D, D)], start=False, stop=True).then_inc(e_y, 1)
            tx(0, 0)
            ahead = {}
            def step(j, s):
                ex = expert_of(nc.tensor, j) if s == 0 and tile_at(j) else ahead.get("hidden")
                if not isinstance(j, int) or j + 1 < SLOTS:
                    tx(j + 1, (s + 1) % RING)
                if tile_at(j):
                    hidden(j, s, ex)
                if s < RING - 1 and tile_at(j + 1):
                    ahead["hidden"] = expert_of(nc.tensor, j + 1)
                if tile_at(j - 2):
                    ex = expert_of(nc.tensor, j - 2)
                if tile_at(j - 1):
                    hidden_T(j - 1, (s - 1) % RING)
                if tile_at(j - 2):
                    down(j - 2, (s - 2) % RING, ex)
            stepped(nc.tensor, step, 2)

        def experts_dve(e, k):
            J = k * SLOTS
            def split(j, s):
                e.wait_ge(e_tx, J + j + 1)
                wait(e, e_h, J + j - 1)
                nc.vector.tensor_copy(XH[s % 2][:, :], bJ[:, 0:128])
                nc.vector.drain()
                nc.vector.tensor_tensor(XL[s % 2][:, :], bJ[:, 0:128], XH[s % 2][:, :], ALU.subtract).then_inc(e_xs, 1)
            def last(j, s):
                e.wait_ge(e_y, J + j + 1)
                if k or not isinstance(j, int) or j >= 4:
                    e.wait_ge(e_sc[s % 4], 16 * (uses(k, j, 4) - 1))
                nc.vector.tensor_copy(out_tok[s % 4][:, :], XS[s][:, TOK:TOK + 1].bitcast(i32))
                nc.vector.scalar_tensor_tensor(OUT[s % 4], bY[:, 0:D], XS[s][:, GATE:GATE + 1], XS[s][:, XX:XX + D],
                                               ALU.mult, ALU.add).then_inc(e_o, 1)
            split(0, 0)
            def step(j, s):
                if not isinstance(j, int) or j + 1 < SLOTS:
                    split(j + 1, (s + 1) % RING)
                if tile_at(j - 2):
                    last(j - 2, (s - 2) % RING)
            stepped(nc.vector, step, 2)

        def experts_act(e, k):
            J = k * SLOTS
            def step(j, s):
                if tile_at(j):
                    e.wait_ge(e_h, J + j + 1)
                    wait(e, e_gt, J + j - 3)
                    nc.scalar.activation(G[s % 4], bS[s % 2][:, :], ACT.Gelu_apprx_tanh).then_inc(e_g, 1)
                if tile_at(j - 1):
                    t = (s - 1) % RING
                    e.wait_ge(e_gt, J + j)
                    wait(e, e_y, J + j - 4)
                    nc.scalar.activation(GT[t % 4], bT[t % 2][:, :], ACT.Copy).then_inc(e_ge, 1)
            stepped(nc.scalar, step, 1)

        def experts_pool(e, k, dst):
            def step(j, s):
                wait_here(e, e_o, k * SLOTS + j + 1)
                nc.gpsimd.indirect_dma_start(
                    dst, bass.IndirectOffsetOnAxis(ap=out_tok[s % 4][:, :], axis=0), OUT[s % 4], None,
                    bounds_check=N - 1, oob_is_err=False).then_inc(e_sc[s % 4], 16)
            stepped(nc.gpsimd, step, 0)
            for s in range(4):
                e.wait_ge(e_sc[s], 16 * (SLOTS // 4) * (k + 1))

        def attention(e, body, middle=None):
            for b in range(1):
                for s in range(2):
                    body(b, s, s, True)
                with e.Fori(1, PAIRS // 2) as k:
                    for s in range(2):
                        body(b, k * 2 + s, s, False)
            with e.Fori(1, B) as b:
                for s in range(2):
                    body(b, s, s, True)
                with e.Fori(1, PAIRS // 2) as k:
                    for s in range(2):
                        body(b, k * 2 + s, s, False)

        def idx(b, p):
            return b * PAIRS + p

        def pe_proj(e, n, which, par, xbatch):
            if which == "q":
                e.wait_ge(ws_ld[par], (n - par) * 8 + 16)
                e.wait_ge(xb_ld, (xbatch + 1) * 16)
            o = 0 if which == "q" else 2
            W = WS[par]
            nc.tensor.matmul(bJ[:, :], W[:, o, :], xTb[:, 0, :], start=True, stop=False)
            nc.tensor.matmul(bJ[:, :], W[:, o, :], xTb[:, 1, :], start=False, stop=False)
            nc.tensor.matmul(bJ[:, :], W[:, o + 1, :], xTb[:, 0, :], start=False, stop=True)\
                .then_inc(s_pq if which == "q" else s_pk, 1)

        def pe_proj_v(pair):
            hi, lo = wvs[:, 0, ds(pair * 128, 128)], wvs[:, 1, ds(pair * 128, 128)]
            for j in range(NJ):
                o_, c = bJ[:, 128 * j:128 * j + 128], slice(128 * j, 128 * j + 128)
                nc.tensor.matmul(o_, xTb[:, 0, c], hi, start=True, stop=False)
                nc.tensor.matmul(o_, xTb[:, 0, c], lo, start=False, stop=False)
                last = nc.tensor.matmul(o_, xTb[:, 1, c], hi, start=False, stop=True)
            last.then_inc(s_pv, 1)

        def pe_scores(e, i, par, g):
            G_ = i * NG + g
            if g == 0:
                e.wait_ge(s_qt, i + 1)
                e.wait_ge(s_kt, i + 1)
            wait(e, s_exp, G_ - 2)
            h = slice(64 * (g // 3), 64 * (g // 3) + 64)
            S = bS[g % 3]
            for qt, c0, nb in SUPER[g % 3]:
                nc.tensor.matmul(S[:, c0:c0 + 128 * nb], QT[par][h, 128 * qt:128 * qt + 128], KT[par][h, 0:128 * nb],
                                 start=True, stop=False)
                last = nc.tensor.matmul(S[:, c0 + 128 * (nb - 1):c0 + 128 * nb], identb[:, :], maskb[:, :],
                                        start=False, stop=True)
            last.then_inc(s_S, 1)

        def pe_PT(e, i, g):
            G_ = i * NG + g
            e.wait_ge(s_exp, G_ + 1)
            wait(e, s_pt, G_ - 1)
            w = sum(nb for _, _, nb in SUPER[g % 3])
            for c in range(w):
                last = nc.tensor.transpose(bT[g % 2][:, 128 * c:128 * c + 128], P[g % 3][:, 128 * c:128 * c + 128], ident[:, :])
            last.then_inc(s_T, 1)

        def pe_AV(e, i, par, g):
            G_ = i * NG + g
            e.wait_ge(s_pt, G_ + 1)
            if g == 0:
                e.wait_ge(s_vr, i + 1)
                wait(e, s_norm, i)
            hh = g // 3
            for qt, c0, nb in SUPER[g % 3]:
                u = 4 * hh + qt
                for kb in range(nb):
                    last = nc.tensor.matmul(bO[:, DH * u:DH * u + DH], PT[g % 2][:, c0 + 128 * kb:c0 + 128 * kb + 128],
                                            V[par][:, kb, DH * hh:DH * hh + DH], start=(kb == 0), stop=(kb == nb - 1))
            last.then_inc(s_av, 1)

        def pe_OT(e, i, par):
            e.wait_ge(s_norm, i + 1)
            for j in range(NJ):
                last = nc.tensor.transpose(bJ[:, 128 * j:128 * j + 128], O[par][:, j, :, :].rearrange("p h d -> p (h d)"), ident[:, :])
            last.then_inc(s_ot, 1)

        def pe_Wo(e, i, pair, batch, final):
            e.wait_ge(s_ote, i + 1)
            first_ = isinstance(pair, int) and pair == 0
            if first_:
                wait(e, s_x2, batch)
            for j in range(NJ):
                last = nc.tensor.matmul(bY[:, 128 * j:128 * j + 128], OT[:, 128 * j:128 * j + 128],
                                        wos[:, ds(pair, 1), :].rearrange("p o d -> p (o d)"),
                                        start=(first_ and j == 0), stop=final, skip_group_check=True)
            last.then_inc(s_wo, 1)

        def pe_prepare(e, m):
            e.wait_ge(l_xn, m + 1)
            pe_norm_T(1, bJ, l_t)

        def pe_attention(e):
            def body(b, p, s, peeled):
                i = idx(b, p)
                n = i + 1
                par, npar = s, 1 - s
                first = isinstance(b, int) and peeled and s == 0
                router = peeled and s == 1 and not isinstance(b, int)
                pe_scores(e, i, par, 2)
                pe_PT(e, i, 0)
                if peeled and s == 1:
                    e.wait_ge(l_lo, b + 2)
                elif first:
                    e.wait_ge(s_vr, 1)
                else:
                    e.wait_ge(s_ote, i - 1)
                pe_proj(e, n, "q", npar, b + (p + 1) // PAIRS)
                pe_scores(e, i, par, 3)
                pe_PT(e, i, 1)
                pe_AV(e, i, par, 0)
                e.wait_ge(s_qr, n + 1)
                pe_proj(e, n, "k", npar, None)
                pe_scores(e, i, par, 4)
                pe_PT(e, i, 2)
                pe_AV(e, i, par, 1)
                e.wait_ge(s_kr, n + 1)
                pe_proj_v((p + 1) % PAIRS)
                pe_scores(e, i, par, 5)
                if not first:
                    e.wait_ge(s_vr, n + 1)
                    pe_OT(e, i - 1, npar)
                pe_PT(e, i, 3)
                pe_AV(e, i, par, 2)
                if router:
                    e.wait_ge(r_xn, b + 8)
                    e.wait_ge(s_ote, i)
                    pe_norm_T(0, bJ, r_t)
                pe_scores(e, n, npar, 0)
                pe_PT(e, i, 4)
                pe_AV(e, i, par, 3)
                if router:
                    pe_logits(e, b + 7, bJ)
                if peeled and s == 0:
                    if not first:
                        e.wait_ge(s_ote, i)
                    else:
                        e.wait_ge(s_vr, n + 1)
                    pe_prepare(e, b + 1)
                pe_scores(e, n, npar, 1)
                pe_PT(e, i, 5)
                pe_AV(e, i, par, 4)
                if not first:
                    if peeled and s == 0:
                        pe_Wo(e, i - 1, PAIRS - 1, b, True)
                    else:
                        pe_Wo(e, i - 1, 0 if peeled else p - 1, b, False)
                pe_AV(e, i, par, 5)
                if router:
                    pe_rank(e, b + 7, bJ)
                    wait_here(e, r_rkr, b + 8)
            pe_prepare(e, 0)
            e.wait_ge(l_lo, 1)
            pe_proj(e, 0, "q", 0, 0)
            e.wait_ge(s_qr, 1)
            pe_proj(e, 0, "k", 0, None)
            e.wait_ge(s_kr, 1)
            pe_proj_v(0)
            pe_scores(e, 0, 0, 0)
            pe_scores(e, 0, 0, 1)
            attention(nc.tensor, body)
            i = B * PAIRS - 1
            e.wait_ge(s_ote, i)
            pe_OT(e, i, 1)
            pe_Wo(e, i, PAIRS - 1, B, True)
            e.wait_ge(r_xn, 8 + B)
            e.wait_ge(s_ote, i + 1)
            pe_norm_T(0, bJ, r_t)
            pe_logits(e, B + 7, bJ)
            e.wait_ge(r_oh, B + 8)
            pe_rank(e, B + 7, bJ)

        def dve_max(e, i, par, g):
            e.wait_ge(s_S, i * NG + g + 1)
            for qt, c0, nb in SUPER[g % 3]:
                u = 4 * (g // 3) + qt
                last = nc.vector.tensor_reduce(nmax[par][:, u:u + 1], bS[g % 3][:, c0:c0 + 128 * nb], AX.X, ALU.max, negate=True)
            last.then_inc(s_max, 1)

        swap = [c ^ 1 for c in range(32)]

        def dve_rope(e, n, which):
            done, free, read, parts = (s_pq, s_qt, s_qr, s_qv) if which == "q" else (s_pk, s_kt, s_kr, s_kv)
            C_, S_, o = (cosq, sinq, 0) if which == "q" else (cosk, sink, 2)
            e.wait_ge(done, n + 1)
            wait(e, free, n)
            nc.vector.tensor_tensor(C_[:, :], bJ[:, :], rope[:, o, :], ALU.mult)
            nc.vector.stream_shuffle(S_[:, :], bJ[:, :], mask=swap).then_inc(read, 1)
            e.wait_ge(read, n + 1)
            nc.vector.tensor_tensor(S_[:, :], S_[:, :], rope[:, o + 1, :], ALU.mult).then_inc(parts, 1)

        def dve_x2(e, b1_):
            e.wait_ge(s_wo, b1_ * PAIRS)
            e.wait_ge(s_bo, b1_)
            x_ = PL[0][:, :, XX:XX + D]
            nc.vector.tensor_tensor(x_, bY[:, :].rearrange("p (j d) -> p j d", j=NJ), x_, ALU.add).then_inc(s_x2, 1)
            nc.vector.drain()
            dve_stats(0, for_router)

        def dve_low(e, m):
            e.wait_ge(l_hi, m + 1)
            nc.vector.tensor_tensor(xTn[:, 1, :], bJ[:, :], xTn[:, 0, :], ALU.subtract).then_inc(l_lo, 1)

        def dve_attention(e):
            def norm(i, par):
                e.wait_ge(s_av, i * NG + NG)
                nc.vector.reciprocal(rinv[:, :], rsum[par][:, :])
                nc.vector.drain()
                nc.vector.tensor_tensor(O[par][:, :, :, :].rearrange("p j h d -> p h j d"),
                                        bO[:, :].rearrange("p (h j d) -> p h j d", h=2, j=NJ),
                                        rinv[:, :].rearrange("p (h j) -> p h j", h=2).unsqueeze(3).broadcast_to([128, 2, NJ, DH]),
                                        ALU.mult).then_inc(s_norm, 1)
            def body(b, p, s, peeled):
                i = idx(b, p)
                n = i + 1
                par, npar = s, 1 - s
                prepare = peeled and s == 0
                router = peeled and s == 1 and not isinstance(b, int)
                dve_max(e, i, par, 2)
                dve_rope(e, n, "q")
                dve_max(e, i, par, 3)
                dve_rope(e, n, "k")
                if prepare:
                    e.wait_ge(x_ld[1], (b + 2) * 16 + 32)
                    dve_stats(1, for_attention)
                if router:
                    dve_x2(e, b)
                dve_max(e, i, par, 4)
                if prepare:
                    dve_norm(e, b + 1, 1, for_attention)
                if router:
                    dve_norm(e, b + 7, 0, for_router)
                dve_max(e, i, par, 5)
                dve_max(e, n, npar, 0)
                if prepare:
                    dve_low(e, b + 1)
                dve_max(e, n, npar, 1)
                if router:
                    dve_route(e, b + 7, bJ)
                norm(i, par)
                if router:
                    dve_position(e, b + 7, b - 1, 0, bJ)
            e.wait_ge(x_ld[1], 48)
            dve_stats(1, for_attention)
            dve_norm(e, 0, 1, for_attention)
            dve_low(e, 0)
            dve_rope(e, 0, "q")
            dve_rope(e, 0, "k")
            dve_max(e, 0, 0, 0)
            dve_max(e, 0, 0, 1)
            attention(nc.vector, body)
            dve_x2(e, B)
            dve_norm(e, B + 7, 0, for_router)
            dve_route(e, B + 7, bJ)
            dve_position(e, B + 7, B - 1, 0, bJ)

        def act_attention(e):
            def exps(i, par, g):
                G_ = i * NG + g
                e.wait_ge(s_max, G_ + 1)
                wait(e, s_T, G_ - 2)
                for qt, c0, nb in SUPER[g % 3]:
                    u = 4 * (g // 3) + qt
                    last = nc.scalar.activation(P[g % 3][:, c0:c0 + 128 * nb], bS[g % 3][:, c0:c0 + 128 * nb], ACT.Exp,
                                                bias=nmax[par][:, u:u + 1], accum_out=rsum[par][:, u:u + 1])
                last.then_inc(s_exp, 1)
            def pt_out(i, g):
                G_ = i * NG + g
                e.wait_ge(s_T, G_ + 1)
                wait(e, s_av, G_ - 1)
                w = 128 * sum(nb for _, _, nb in SUPER[g % 3])
                nc.scalar.activation(PT[g % 2][:, 0:w], bT[g % 2][:, 0:w], ACT.Copy).then_inc(s_pt, 1)
            def v_out(n, par):
                e.wait_ge(s_pv, n + 1)
                wait(e, s_av, (n - 1) * NG)
                nc.scalar.activation(V[par][:, :, :], bJ[:, :].rearrange("p (j d) -> p j d", j=NJ), ACT.Copy).then_inc(s_vr, 1)
            def ot_out(i):
                e.wait_ge(s_ot, i + 1)
                wait(e, s_wo, i)
                nc.scalar.activation(OT[:, :], bJ[:, :], ACT.Copy).then_inc(s_ote, 1)
            def high_(m):
                e.wait_ge(l_t, m + 1)
                wait(e, xb_ld, m * 16)
                nc.scalar.activation(xTn[:, 0, :], bJ[:, :], ACT.Copy).then_inc(l_hi, 1)
            def body(b, p, s, peeled):
                i = idx(b, p)
                n = i + 1
                par, npar = s, 1 - s
                first = isinstance(b, int) and peeled and s == 0
                router = peeled and s == 1 and not isinstance(b, int)
                for g in range(NG):
                    if g < NG - 1:
                        exps(i, par, g + 1)
                    else:
                        exps(n, npar, 0)
                    if g == 4 and router:
                        act_xT(e, b + 7, bJ)
                    pt_out(i, g)
                    if g == 2:
                        v_out(n, npar)
                    if g == 3 and not first:
                        ot_out(i - 1)
                    if g == 4 and peeled and s == 0:
                        high_(b + 1)
                if router:
                    act_exp(e, b + 7)
            high_(0)
            v_out(0, 0)
            exps(0, 0, 0)
            attention(nc.scalar, body)
            ot_out(B * PAIRS - 1)
            act_xT(e, B + 7, bJ)
            act_exp(e, B + 7)

        def pool_attention(e):
            def add(n, par, which):
                parts, done, dst, C_, S_ = (s_qv, s_qt, QT, cosq, sinq) if which == "q" else (s_kv, s_kt, KT, cosk, sink)
                e.wait_ge(parts, n + 1)
                wait(e, s_S, (n - 1) * NG)
                nc.gpsimd.tensor_tensor(dst[par][:, :], C_[:, :], S_[:, :], ALU.add).then_inc(done, 1)
            def bias(b):
                e.wait_ge(x_ld[0], b * 16 + 48)
                for j in range(NJ):
                    last = nc.gpsimd.tensor_tensor(PL[0][:, j, XX:XX + D], PL[0][:, j, XX:XX + D], bo_bc[:, :], ALU.add)
                last.then_inc(s_bo, 1)
            def body(b, p, s, peeled):
                i = idx(b, p)
                router = peeled and s == 1 and not isinstance(b, int)
                add(i + 1, 1 - s, "q")
                add(i + 1, 1 - s, "k")
                if peeled and s == 0:
                    pool_rstd(e, b + 1, for_attention)
                    if not isinstance(b, int):
                        bias(b - 1)
                if router:
                    pool_rstd(e, b + 7, for_router)
                    pool_scatter(e, b + 7, 0)
            pool_rstd(e, 0, for_attention)
            add(0, 0, "q")
            add(0, 0, "k")
            attention(nc.gpsimd, body)
            bias(B - 1)
            pool_rstd(e, B + 7, for_router)
            pool_scatter(e, B + 7, 0)

        def sp_attention(e):
            def load_w(n, par, pair):
                wait_here(e, s_pk, n - 1)
                e.dma_start(WS[par][:, :, :].bitcast(f32), wqk[:, :, ds(pair * 128, 128)].bitcast(f32)).then_inc(ws_ld[par], 16)
            def next_x(m):
                wait_here(e, s_pv, m * PAIRS)
                wait_here(e, l_lo, m + 1)
                e.dma_start(xTb[:, :, :].bitcast(f32), xTn[:, :, :].bitcast(f32)).then_inc(xb_ld, 16)
            def tokens_of(m, batch):
                wait_here(e, l_t, m)
                e.dma_start(PL[1][:, :, XX:XX + D], xrows(x1, batch)).then_inc(x_ld[1], 16)
            tokens_of(0, 0)
            load_w(0, 0, 0)
            load_w(1, 1, 1)
            next_x(0)
            def residual(b):
                wait_here(e, r_sc[0], b * 64 + 128)
                e.dma_start(PL[0][:, :, XX:XX + D], xrows(x1, b)).then_inc(x_ld[0], 16)
            def batch(b):
                tokens_of(b + 1, (b + 1) % B)
                with nc.sync.Fori(0, PAIRS // 2 - 1) as k:
                    for s in range(2):
                        load_w(idx(b, k * 2 + s + 2), s, k * 2 + s + 2)
                residual(b)
                for s in range(2):
                    load_w(idx(b, PAIRS + s), s, s)
                next_x(b + 1)
            batch(0)
            with nc.sync.Fori(1, B) as b:
                batch(b)

        block = ctx.enter_context(nc.Block())

        @block.sync
        def _(sp):
            def tokens_in(b):
                par = b % NPL
                if b >= NPL:
                    sp.wait_ge(r_sc[par], 64 * (b // NPL))
                sp.dma_start(PL[par][:, :, XX:XX + D], xrows(x, b)).then_inc(x_ld[par], 16)
            tokens_in(0)
            for dst, src in ((ident, c_ident), (small, c_small), (swt, sw),
                             (sbias, sb_.rearrange("(o j e) -> o j e", o=1, j=1).broadcast_to([128, NJ, EX]))):
                sp.dma_start(dst[:], src).then_inc(c_ld, 16)
            for b in range(1, NPL):
                tokens_in(b)
            for dst, src in ((slot_c, c_slots), (bo_bc, bo.rearrange("(o d) -> o d", o=1).broadcast_to([128, D])),
                             (rope, c_rope)):
                sp.dma_start(dst[:], src).then_inc(c_ld2, 16)
            for b in range(NPL, B):
                tokens_in(b)
            sp.wait_ge(prep, 1)
            for s_ in range(SPARE):
                r0 = EX * REGION + s_ * TILE
                sp.dma_start(region[r0:r0 + TILE, :], pad[:, :]).then_inc(spare_st, 16)
            sp_pads(sp, 0, [128] * NPL)
            experts_sp(sp, 0)
            all_meet(sp, 1)
            sp_attention(sp)
            sp_pads(sp, 1, [128 + 64 * B, 128, 128, 128])
            all_meet(sp, 2)
            experts_sp(sp, 1)
            all_meet(sp, 3)

        @block.scalar
        def _(act):
            act.dma_start(bias_raw[:, 0:32], b1.rearrange("e (a c) -> (e a) c", c=32)).then_inc(w2_ld, 16)
            act.dma_start(bias_raw[:, 32:40], b2.rearrange("e (a c) -> (e a) c", c=8)).then_inc(w2_ld, 16)
            act.dma_start(w2s[:, :, :, :], w2.rearrange("e (c p) d -> p e c d", p=128)).then_inc(w2_ld, 16)
            act.dma_start(wos[:, :, :], wo.rearrange("(a p) d -> p a d", p=128)).then_inc(w2_ld, 16)
            for c in range(2):
                act.dma_start(raw[c][:, :], chunks[c][0]).then_inc(raw_ld[c], 16)
            def high(c):
                act.wait_ge(raw_ld[c % 2], 16 * (c // 2 + 1))
                nc.scalar.activation(chunks[c][1], raw[c % 2][:, :], ACT.Copy).then_inc(raw_hi, 1)
                if c + 1 >= 2 and c + 1 < NCH:
                    act.wait_ge(raw_lo, c)
                    act.dma_start(raw[(c + 1) % 2][:, :], chunks[c + 1][0]).then_inc(raw_ld[(c + 1) % 2], 16)
            act.wait_ge(w2_ld, 64)
            nc.scalar.activation(bias_hl[:, 0, :], bias_raw[:, :], ACT.Copy).then_inc(bias_hi, 1)
            high(0)
            for b in range(B):
                act_xT(act, b, bJ)
                act_exp(act, b)
                if b < NCH - 1:
                    high(b + 1)
            for c in range(B + 1, NCH):
                high(c)
            experts_act(act, 0)
            all_meet(act, 1)
            act_attention(act)
            all_meet(act, 2)
            experts_act(act, 1)
            all_meet(act, 3)

        @block.gpsimd
        def _(pool):
            nc.gpsimd.memset(pad[:, :], 0.0)
            pool.drain()
            nc.gpsimd.memset(pad[:, TOK:TOK + 1].bitcast(i32), NOWHERE)
            nc.gpsimd.iota(tokens[:, :], [[TILE, N // TILE]], base=0, channel_multiplier=1)
            nc.gpsimd.memset(onesb[:, :], 1.0)
            nc.gpsimd.memset(mhalf[:, :], -0.5)
            nc.gpsimd.memset(onesr[:, :].bitcast(f32), 1.0)
            nc.gpsimd.dma_start(identb[:, :], c_ident).then_inc(bias_ld, 16)
            nc.gpsimd.dma_start(maskb[:, :], c_mask).then_inc(bias_ld, 16)
            nc.gpsimd.dma_start(upperb[:, :], c_upper).then_inc(bias_ld, 16)
            pool.drain().then_inc(prep, 1)
            pool.wait_ge(bias_hi, 1)
            nc.gpsimd.tensor_tensor(bias_hl[:, 1, :], bias_raw[:, :], bias_hl[:, 0, :], ALU.subtract)
            pool.drain()
            for r in range(2):
                nc.gpsimd.dma_start(b1s[r:r + 1, :].rearrange("o (a c) -> o a c", c=32).bitcast(f32), bias_hl[:, r, 0:32].bitcast(f32)).then_inc(bias_ld, 16)
                nc.gpsimd.dma_start(b2s[r:r + 1, :].rearrange("o (a c) -> o a c", c=8).bitcast(f32), bias_hl[:, r, 32:40].bitcast(f32)).then_inc(bias_ld, 16)
            def low(c):
                pool.wait_ge(raw_hi, c + 1)
                nc.gpsimd.tensor_tensor(chunks[c][2], raw[c % 2][:, :], chunks[c][1], ALU.subtract).then_inc(raw_lo, 1)
            pool_rstd(pool, 0, for_router)
            for b in range(B):
                if b + 1 < B:
                    pool_rstd(pool, b + 1, for_router)
                low(b)
                pool_scatter(pool, b, b % NPL)
            for c in range(B, NCH):
                low(c)
            experts_pool(pool, 0, x1)
            all_meet(pool, 1)
            pool.wait_ge(c_ld2, 48)
            pool_attention(pool)
            all_meet(pool, 2)
            experts_pool(pool, 1, out)
            all_meet(pool, 3)

        @block.vector
        def _(dve):
            nc.vector.memset(cum[:, :], 0.0)
            dve.wait_ge(c_ld, 64)
            dve.wait_ge(prep, 1)
            dve.wait_ge(x_ld[0], 16)
            dve_stats(0, for_router)
            dve_norm(dve, 0, 0, for_router)
            for b in range(B):
                if b + 1 < B:
                    par = (b + 1) % NPL
                    dve.wait_ge(x_ld[par], 16 * ((b + 1) // NPL + 1))
                    dve_stats(par, for_router)
                dve_route(dve, b, bY)
                if b + 1 < B:
                    dve_norm(dve, b + 1, par, for_router)
                dve_position(dve, b, b, b % NPL, bO)
            dve.wait_ge(c_ld2, 48)
            dve.drain()
            dve_table(dve, 0)
            experts_dve(dve, 0)
            all_meet(dve, 1)
            nc.vector.memset(cum[:, :], 0.0)
            dve_attention(dve)
            dve.drain()
            dve_table(dve, 1)
            all_meet(dve, 2)
            experts_dve(dve, 1)
            all_meet(dve, 3)

        @block.tensor
        def _(pe):
            pe.wait_ge(c_ld, 64)
            pe.wait_ge(bias_ld, 112)
            pe.wait_ge(prep, 1)
            for b in range(B):
                pe.wait_ge(r_xn, b + 1)
                wait(pe, r_xt, b)
                pe_norm_T(b % NPL, bJ, r_t)
                pe_logits(pe, b, bY)
                pe_rank(pe, b, bO)
            pe_counts(pe, 0)
            pe.wait_ge(r_tab, 1)
            pe.wait_ge(raw_lo, EX)
            pe.wait_ge(w2_ld, 64)
            experts_pe(pe, 0)
            all_meet(pe, 1)
            pe.wait_ge(raw_lo, NCH)
            pe_attention(pe)
            pe_counts(pe, 1)
            all_meet(pe, 2)
            experts_pe(pe, 1)
            all_meet(pe, 3)


_INS = ["L0_attn_x", "L0_attn_Wq", "L0_attn_Wk", "L0_attn_Wv", "L0_attn_Wo", "L0_attn_bo",
        "L0_ffn_switch_w", "L0_ffn_switch_b", "L0_ffn_w1", "L0_ffn_b1", "L0_ffn_w2", "L0_ffn_b2"]


def _constants():
    f = np.float32
    p = np.arange(128)
    inv = (1.0 / 10000.0 ** (np.arange(0, DH, 2, dtype=f) / f(DH))).astype(f)
    ang = (np.arange(T, dtype=f)[:, None] * inv[None, :]).astype(f)
    cos = np.cos(ang).astype(f)[:, (p % DH) // 2].T
    sin = np.sin(ang).astype(f)[:, (p % DH) // 2].T * np.where(p % 2 == 0, -1, 1)[:, None].astype(f)
    scale = f(DH ** -0.5)
    rope = np.stack([cos * scale, sin * scale, cos, sin], 1).astype(f)
    e = np.arange(EX, dtype=f)
    small = np.zeros((128, 2, NJ, EX), f)
    small[:, 0], small[:, 1] = EX - e, e * REGION
    s = np.arange(SLOTS, dtype=f)
    slots = np.concatenate([s * TILE, np.repeat(s, EX), (e[None, :] <= e[:, None]).astype(f).ravel(),
                            np.tile(np.arange(32, dtype=f) * TILE, EX)])[None]
    return {
        "ident": np.eye(128, dtype=f),
        "mask": np.where(p[None, :] > p[:, None], MASKED, 0).astype(f),
        "upper": (p[:, None] < p[None, :]).astype(f),
        "rope": rope, "small": small, "slots": slots.astype(f),
    }


def kernel(**inputs):
    import concourse.bacc as _bacc
    from concourse.bass_utils import run_bass_kernel_spmd as _run

    nc = _bacc.Bacc("TRN2", target_bir_lowering=False, num_devices=1)
    arrays, args = {}, []

    def given(name, a):
        a = np.ascontiguousarray(a)
        arrays[name] = a
        args.append(nc.dram_tensor(name, a.shape, mybir.dt.from_np(a.dtype), kind="ExternalInput").ap())

    for name in _INS:
        a = np.asarray(inputs[name])
        if name == "L0_attn_x":
            a = a.reshape(N, D)
        given(f"in_{name}", a)
    for name, a in _constants().items():
        given(f"const_{name}", a)
    out = nc.dram_tensor("out_0", (N, D), mybir.dt.float32, kind="ExternalOutput").ap()
    macaron_kernel(nc, *args, out)
    r = _run(nc, [arrays], core_ids=[0])
    return np.asarray(r.results[0]["out_0"]).reshape(B, T, D)
```

```python
from contextlib import ExitStack

import numpy as np

import concourse.bass as bass
from concourse import mybir

B, T, D = 8, 512, 128
TILE = 128
NJ = T // TILE
N = B * T
HEADS, DH = 16, 64
PAIRS = HEADS // 2
EX, F = 8, 512
FC = F // 128
RING = 8
SLOTS = -(-(N // TILE + EX - 1) // RING) * RING
REGION = N + TILE
SPARE = SLOTS - N // TILE
ROWS = EX * REGION + SPARE * TILE
XN, XX, GATE, TOK, ROW = 0, D, 2 * D, 2 * D + 1, 2 * D + 2
NOWHERE = 1 << 20
NPL = B
NRAW = 4
PEELED = 4
LN = [0, 1, B // 2, B]
LN_AFTER = len(LN) - 2
EPS = 1e-5
MASKED = -1e30
SUPER = [[(3, 0, 4)], [(0, 0, 1), (2, 128, 3)], [(1, 0, 2)]]
NG = 2 * len(SUPER)


def macaron_kernel(nc, x, wq, wk, wv, wo, bo, sw, sb_, w1, b1, w2, b2,
                   c_ident, c_mask, c_upper, c_rope, c_small, c_slots, out):
    f32, f32r, bf16, i32 = mybir.dt.float32, mybir.dt.float32r, mybir.dt.bfloat16, mybir.dt.int32
    ALU, ACT, AX = mybir.AluOpType, mybir.ActivationFunctionType, mybir.AxisListType
    ds = bass.ds
    ctx = ExitStack()
    with ctx:
        def sb(name, shape, dt=f32):
            return ctx.enter_context(nc.sbuf_tensor(name, shape, dt))

        def sem(name):
            return ctx.enter_context(nc.semaphore(name))

        region = nc.dram_tensor("routed_rows", [ROWS, ROW], f32).ap()
        x1 = nc.dram_tensor("x_after_ffn1", [N, D], f32).ap()

        ident = sb("ident", [128, 128])
        identb = sb("identb", [128, 128], bf16)
        maskb = sb("maskb", [128, 128], bf16)
        upperb = sb("upperb", [128, 128], bf16)
        onesb = sb("onesb", [128, 128], bf16)
        onesr = sb("onesr", [2, 128], f32r)
        rope = sb("rope", [128, 4, T])
        small = sb("small", [128, 2, NJ, EX])
        sbias = sb("sbias", [128, NJ, EX])
        slot_c = sb("slot_c", [1, SLOTS + SLOTS * EX + EX * EX + EX * 32])
        tokens = sb("tokens", [128, N // TILE], i32)
        bo_bc = sb("bo_bc", [128, D])
        swt = sb("swt", [128, EX])
        w1s = sb("w1s", [128, 2, EX * F], f32r)
        w2s = sb("w2s", [128, EX, FC, D])
        b1s = sb("b1s", [2, EX * F], f32r)
        b2s = sb("b2s", [2, EX * D], f32r)
        wqk = sb("wqk", [128, 4, HEADS * DH], f32r)
        wvs = sb("wvs", [128, 2, HEADS * DH], f32r)
        wos = sb("wos", [128, PAIRS, D])

        raw = [sb(f"raw{i}", [128, 512]) for i in range(NRAW)]
        bias_hl = sb("bias_hl", [128, 2, 40], f32r)
        bias_raw = sb("bias_raw", [128, 40])
        PL = [sb(f"payload{i}", [128, NJ, ROW]) for i in range(NPL)]
        pad = sb("pad", [128, ROW])
        stats = sb("stats", [128, 2, NJ, 6])
        mv = sb("mv", [128, B, NJ, 2])
        var = sb("var", [128, B, NJ])
        rstd = sb("rstd", [128, B, NJ])
        mhalf = sb("mhalf", [128, B, NJ])
        xT = sb("xT", [128, T])
        lg = sb("lg", [128, NJ, EX])
        lmax = sb("lmax", [128, NJ])
        ldiff = sb("ldiff", [128, NJ, EX])
        lexp = sb("lexp", [128, NJ, EX])
        lsum = sb("lsum", [128, NJ])
        eq = sb("eq", [128, NJ, EX])
        first = sb("first", [128, NJ])
        oh = sb("oh", [128, NJ, EX])
        ohb = sb("ohb", [128, NJ, EX], bf16)
        ohsum = sb("ohsum", [128, EX])
        cum = sb("cum", [128, EX])
        cumb = sb("cumb", [128, EX], bf16)
        rk = sb("rk", [128, NJ, EX])
        posf = sb("posf", [128, NJ])
        pos = [sb(f"pos{i}", [128, NJ], i32) for i in range(NPL)]
        cnt = sb("cnt", [1, EX])
        tiles_e = sb("tiles_e", [1, EX])
        tri = sb("tri", [1, EX, EX])
        ends = sb("ends", [1, EX])
        skip = sb("skip", [1, EX])
        sl_e = sb("sl_e", [1, SLOTS])
        sl_r = sb("sl_r", [1, SLOTS])
        slot_expert = sb("slot_expert", [1, SLOTS], i32)
        slot_row = sb("slot_row", [1, SLOTS], i32)
        pad_row = sb("pad_row", [1, EX], i32)
        QD = [sb(f"q_stack{i}", [128, 2, T], f32r) for i in range(2)]
        KD = [sb(f"k_stack{i}", [128, 2, 2, T], f32r) for i in range(2)]
        spare = [PL[i][:, :, :].rearrange("p j c -> p (j c)")[:, 512 * h:512 * h + 512] for i in range(2, NPL) for h in range(2)]
        cosq, sinq, cosk, sink = spare[0:4]
        RQ, RK = spare[11], raw[0][:, :]
        QH, QL = [raw[i][:, :].bitcast(f32r) for i in (1, 2)]
        P = [sb(f"P{i}", [128, 512]) for i in range(3)]
        ge, ge2 = [P[i][0:1, 0:SLOTS * EX].rearrange("p (s e) -> p s e", e=EX) for i in range(2)]
        cmp32 = P[2][0:1, 0:EX * 32].rearrange("p (e s) -> p e s", s=32)
        PT, flatV, flatO, OT = spare[4:6], spare[6:8], spare[8:10], spare[10]
        V = [t.rearrange("p (j d) -> p j d", j=NJ) for t in flatV]
        O = [t.rearrange("p (j h d) -> p j h d", j=NJ, h=2) for t in flatO]
        WS = [sb(f"WS{i}", [128, 4, 128], f32r) for i in range(2)]
        xTb = sb("xTb", [128, 2, T], f32r)
        xTn = sb("xTn", [128, 2, T], f32r)
        nmax = [sb(f"nmax{i}", [128, 8]) for i in range(2)]
        rsum = [sb(f"rsum{i}", [128, 8]) for i in range(2)]
        rinv = sb("rinv", [128, 8])
        XS = [t[:, 0:ROW] for t in (RQ, xT, sinq, cosk, *flatV)] + [sb("rows6", [128, ROW])[:, :], sb("rows7", [128, ROW])[:, :]]
        XH = [sb(f"xh{i}", [128, 128], f32r) for i in range(2)]
        XL = [sb(f"xl{i}", [128, 128], f32r) for i in range(2)]
        G = [P[0][:, :], P[1][:, :], P[2][:, :], flatO[0]]
        GT = [PT[0][:, :], PT[1][:, :], cosq[:, :], sink[:, :]]
        OUT = [OT[:, 128 * i:128 * i + 128] for i in range(4)]
        out_tok = [sb(f"out_tok{i}", [128, 1], i32) for i in range(4)]

        bank = [ctx.enter_context(nc.psum_tensor(f"bank{i}", [128, 512], f32)) for i in range(8)]
        bS, bT, bJ, bO, bY = bank[0:3], bank[3:5], bank[5], bank[6], bank[7]

        c_ld, c_ld2, raw_hi, raw_lo = [sem(n) for n in ("consts_loaded", "late_consts_loaded", "raw_high", "raw_low")]
        raw_ld = [sem(f"raw_loaded{i}") for i in range(NRAW)]
        prep, bias_hi, bias_in, bias_ld, bf_ld, w2_ld = [sem(n) for n in (
            "prep", "bias_high", "biases_loaded", "bias_rows", "bf16_consts_loaded", "w2_loaded")]
        spare_st = sem("spare_rows_stored")
        x_ld = [sem(f"x_loaded{i}") for i in range(NPL)]
        r_sc = [sem(f"rows_scattered{i}") for i in range(NPL)]
        r_var, r_rstd, r_xn, r_t, r_xt, r_lg, r_d, r_ex, r_oh, r_rk, r_rkr, r_pos, r_cnt, r_prow, r_tab, r_pad = [sem("router_" + n) for n in (
            "var", "rstd", "normed", "transposed", "xT", "logits", "diff", "exp", "onehot", "rank", "rank_read", "pos", "counts", "pad_rows", "table", "padded")]
        e_ld = [sem(f"tile_loaded{i}") for i in range(RING)]
        e_sc = [sem(f"tile_scattered{i}") for i in range(4)]
        e_tx, e_xs, e_h, e_g, e_gt, e_ge, e_y, e_o = [sem("expert_" + n) for n in (
            "xT", "xsplit", "hidden", "gelu", "hiddenT", "hiddenT_out", "y", "out")]
        l_var, l_rstd, l_xn, l_t, l_hi, l_lo = [sem("ln_" + n) for n in (
            "var", "rstd", "normed", "transposed", "high", "low")]
        ws_ld = [sem("ws_loaded0"), sem("ws_loaded1")]
        xb_ld, tick, phase = sem("xTb_loaded"), sem("tick"), sem("phase")
        s_pq, s_pk, s_pv, s_qr, s_kr, s_vr, s_qt, s_kt, s_qh, s_kh, s_ql, s_kl = [sem("a_" + n) for n in (
            "proj_q", "proj_k", "proj_v", "q_read", "k_read", "v_read", "q_roped", "k_roped", "q_high", "k_high", "q_low", "k_low")]
        qk_ld = [sem("qk_stacked0"), sem("qk_stacked1")]
        s_S, s_max, s_exp, s_T, s_pt, s_av, s_norm, s_ot, s_ote, s_wo, s_x2, s_bo = [sem("a_" + n) for n in (
            "scores", "max", "exp", "PT", "PT_out", "AV", "norm", "OT", "OT_out", "wo", "x2", "bo")]

        def wait(e, s, v):
            if not isinstance(v, int) or v > 0:
                e.wait_ge(s, v)

        def wait_here(e, s, v):
            wait(e, s, v)
            e.sem_inc(tick, 1)

        def all_meet(e, k):
            e.drain().then_inc(phase, 1)
            e.wait_ge(phase, 5 * k)

        chunks = [(w1[e], w1s[:, 0, e * F:(e + 1) * F], w1s[:, 1, e * F:(e + 1) * F]) for e in range(EX)]
        for w, dst, k in ((wq, wqk, 0), (wk, wqk, 2), (wv, wvs, 0)):
            for h in range(2):
                cols = slice(512 * h, 512 * h + 512)
                chunks.append((w[:, cols], dst[:, k, cols], dst[:, k + 1, cols]))
        NCH = len(chunks)

        def xrows(src, b):
            return src.rearrange("(b j p) d -> b p j d", p=TILE, j=NJ)[ds(b, 1)].rearrange("o p j d -> p (o j) d")

        for_router, for_attention = (r_var, r_rstd, r_xn), (l_var, l_rstd, l_xn)

        def pool_rstd(e, m, use, at=0, to=1):
            e.wait_ge(use[0], m + 1)
            nc.gpsimd.tensor_tensor(rstd[:, at:to, :], var[:, at:to, :], mhalf[:, at:to, :], ALU.pow).then_inc(use[1], 1)

        def dve_stats(par, at=0):
            for j in range(NJ):
                nc.vector.bn_stats(stats[:, at % 2, j, :], PL[par][:, j, XX:XX + D])
            nc.vector.drain()
            for j in range(NJ):
                nc.vector.bn_aggr(mv[:, at, j, :], stats[:, at % 2, j, :])

        def dve_var(use, at=0, to=1):
            nc.vector.drain()
            nc.vector.tensor_scalar(var[:, at:to, :], mv[:, at:to, :, 1], EPS, None, ALU.add).then_inc(use[0], 1)

        def dve_norm(e, m, par, use, at=0):
            wait(e, use[1], m + 1)
            for j in range(NJ):
                last = nc.vector.tensor_scalar(PL[par][:, j, XN:XN + D], PL[par][:, j, XX:XX + D],
                                               mv[:, at, j, 0:1], rstd[:, at, j:j + 1], ALU.subtract, ALU.mult)
            last.then_inc(use[2], 1)

        def pe_norm_T(par, bankT, done):
            for j in range(NJ):
                last = nc.tensor.transpose(bankT[:, 128 * j:128 * j + 128], PL[par][:, j, XN:XN + D], ident[:, :])
            last.then_inc(done, 1)

        def act_xT(e, n, bankT):
            e.wait_ge(r_t, n + 1)
            wait(e, r_lg, n)
            nc.scalar.activation(xT[:, :], bankT[:, :], ACT.Copy).then_inc(r_xt, 1)

        def pe_logits(e, n, bankL):
            e.wait_ge(r_xt, n + 1)
            for j in range(NJ):
                last = nc.tensor.matmul(bankL[:, EX * j:EX * j + EX], xT[:, 128 * j:128 * j + 128], swt[:, :],
                                        start=True, stop=True)
            last.then_inc(r_lg, 1)

        def dve_route(e, n, bankL):
            V_ = nc.vector
            e.wait_ge(r_lg, n + 1)
            V_.tensor_tensor(lg[:, :, :], bankL[:, 0:NJ * EX].rearrange("p (j e) -> p j e", j=NJ), sbias[:, :, :], ALU.add)
            V_.drain()
            V_.tensor_reduce(lmax[:, :], lg[:, :, :], AX.X, ALU.max)
            V_.drain()
            top = lmax[:, :].unsqueeze(2).broadcast_to([128, NJ, EX])
            V_.tensor_tensor(ldiff[:, :, :], lg[:, :, :], top, ALU.subtract).then_inc(r_d, 1)
            V_.tensor_tensor(eq[:, :, :], lg[:, :, :], top, ALU.is_equal)
            V_.drain()
            V_.tensor_tensor(eq[:, :, :], eq[:, :, :], small[:, 0], ALU.mult)
            V_.drain()
            V_.tensor_reduce(first[:, :], eq[:, :, :], AX.X, ALU.max)
            V_.drain()
            V_.tensor_tensor(oh[:, :, :], small[:, 0], first[:, :].unsqueeze(2).broadcast_to([128, NJ, EX]), ALU.is_equal)
            V_.drain()
            V_.tensor_copy(ohb[:, :, :], oh[:, :, :])
            V_.tensor_copy(cumb[:, :], cum[:, :]).then_inc(r_oh, 1)

        def act_exp(e, n):
            e.wait_ge(r_d, n + 1)
            nc.scalar.activation(lexp[:, :, :], ldiff[:, :, :], ACT.Exp).then_inc(r_ex, 1)

        def pe_rank(e, n, bankR):
            e.wait_ge(r_oh, n + 1)
            R = bankR[:, 0:NJ * EX]
            nc.tensor.matmul(R, onesb[:, :], cumb[:, :].unsqueeze(1).broadcast_to([128, NJ, EX]), start=True, stop=False)
            for j in range(NJ - 1):
                nc.tensor.matmul(bankR[:, EX * (j + 1):NJ * EX], onesb[:, :],
                                 ohb[:, j:j + 1, :].broadcast_to([128, NJ - 1 - j, EX]), start=False, stop=False)
            nc.tensor.matmul(R, upperb[:, :], ohb[:, :, :], start=False, stop=True).then_inc(r_rk, 1)

        def dve_position(e, n, b, par, bankR):
            V_ = nc.vector
            e.wait_ge(r_rk, n + 1)
            V_.tensor_tensor(rk[:, :, :], bankR[:, 0:NJ * EX].rearrange("p (j e) -> p j e", j=NJ), small[:, 1], ALU.add)\
                .then_inc(r_rkr, 1)
            V_.tensor_reduce(ohsum[:, :], oh[:, :, :].rearrange("p j e -> p e j"), AX.X, ALU.add)
            V_.drain()
            V_.tensor_tensor(rk[:, :, :], rk[:, :, :], oh[:, :, :], ALU.mult)
            V_.tensor_tensor(cum[:, :], cum[:, :], ohsum[:, :], ALU.add)
            V_.drain()
            V_.tensor_reduce(posf[:, :], rk[:, :, :], AX.X, ALU.add)
            e.wait_ge(r_ex, n + 1)
            V_.tensor_reduce(lsum[:, :], lexp[:, :, :], AX.X, ALU.add)
            V_.drain()
            V_.reciprocal(lsum[:, :], lsum[:, :])
            V_.tensor_copy(PL[par][:, :, TOK:TOK + 1].bitcast(i32).rearrange("p j o -> p (j o)"), tokens[:, ds(b * NJ, NJ)])
            V_.drain()
            V_.tensor_scalar(PL[par][:, :, GATE], lsum[:, :], 0.5, None, ALU.mult)
            V_.tensor_copy(pos[par][:, :], posf[:, :]).then_inc(r_pos, 1)

        def pool_scatter(e, n, par):
            wait_here(e, r_pos, n + 1)
            for j in range(NJ):
                nc.gpsimd.indirect_dma_start(region, bass.IndirectOffsetOnAxis(ap=pos[par][:, j:j + 1], axis=0),
                                             PL[par][:, j, :], None).then_inc(r_sc[par], 16)

        def pe_counts(e, k):
            e.wait_ge(r_cnt, 2 * k + 1)
            nc.tensor.matmul(bY[:, 0:EX], onesb[:, :], cumb[:, :], start=True, stop=True).then_inc(r_cnt, 1)

        def dve_table(e, k):
            V_ = nc.vector
            o = 0
            jota = slot_c[:, o:o + SLOTS]; o += SLOTS
            jb = slot_c[:, o:o + SLOTS * EX].rearrange("p (s e) -> p s e", e=EX); o += SLOTS * EX
            low = slot_c[:, o:o + EX * EX].rearrange("p (a c) -> p a c", c=EX); o += EX * EX
            steps = slot_c[:, o:o + EX * 32].rearrange("p (e s) -> p e s", s=32)
            V_.tensor_copy(cumb[:, :], cum[:, :]).then_inc(r_cnt, 1)
            e.wait_ge(r_cnt, 2 * k + 2)
            V_.tensor_copy(cnt[:, :], bY[0:1, 0:EX])
            V_.drain()
            V_.tensor_tensor(cmp32[:, :, :], steps, cnt[:, :].unsqueeze(2).broadcast_to([1, EX, 32]), ALU.is_lt)
            V_.tensor_tensor(skip[:, :], cnt[:, :], small[0:1, 1, 0, :], ALU.add)
            V_.drain()
            V_.tensor_copy(pad_row[:, :], skip[:, :]).then_inc(r_prow, 1)
            V_.tensor_reduce(tiles_e[:, :], cmp32[:, :, :], AX.X, ALU.add)
            V_.drain()
            V_.tensor_tensor(tri[:, :, :], low, tiles_e[:, :].unsqueeze(1).broadcast_to([1, EX, EX]), ALU.mult)
            V_.tensor_scalar(skip[:, :], tiles_e[:, :], -float(TILE), float(REGION), ALU.mult, ALU.add)
            V_.drain()
            V_.tensor_reduce(ends[:, :], tri[:, :, :], AX.X, ALU.add)
            V_.drain()
            V_.tensor_tensor(ge[:, :, :], jb, ends[:, :].unsqueeze(1).broadcast_to([1, SLOTS, EX]), ALU.is_ge)
            V_.drain()
            V_.tensor_reduce(sl_e[:, :], ge[:, :, :], AX.X, ALU.add)
            V_.tensor_tensor(ge2[:, :, :], ge[:, :, :], skip[:, :].unsqueeze(1).broadcast_to([1, SLOTS, EX]), ALU.mult)
            V_.drain()
            V_.tensor_reduce(sl_r[:, :], ge2[:, :, :], AX.X, ALU.add)
            V_.tensor_scalar(sl_e[:, :], sl_e[:, :], float(EX - 1), None, ALU.min)
            V_.drain()
            V_.tensor_tensor(sl_r[:, :], sl_r[:, :], jota, ALU.add)
            V_.tensor_copy(slot_expert[:, :], sl_e[:, :])
            V_.drain()
            V_.tensor_copy(slot_row[:, :], sl_r[:, :]).then_inc(r_tab, 1)

        def pads(e, engine, k, experts):
            e.wait_ge(r_prow, k + 1)
            for x_ in experts:
                row = engine.value_load(pad_row[0:1, x_:x_ + 1], min_val=0, max_val=EX * REGION - TILE)
                e.dma_start(region[ds(row, TILE), :], pad[:, :]).then_inc(r_pad, 16)

        def stepped(engine, step, lag):
            for j in range(RING):
                step(j, j)
            with engine.Fori(1, SLOTS // RING - 1) as t:
                for s in range(RING):
                    step(t * RING + s, s)
            for j in range(SLOTS - RING, SLOTS + lag):
                step(j, j % RING)

        def tile_at(j, lo=0):
            return not isinstance(j, int) or lo <= j < SLOTS

        def uses(k, j, ring):
            return j // ring + (k * (SLOTS // ring) + 1)

        def expert_of(engine, j):
            return engine.value_load(slot_expert[0:1, ds(j, 1)], min_val=0, max_val=EX - 1)

        def experts_sp(e, k, scattered):
            e.wait_ge(r_tab, k + 1)
            for par in range(NPL):
                e.wait_ge(r_sc[par], scattered[par])
            e.wait_ge(r_pad, 16 * EX * (k + 1))
            if k == 0:
                e.wait_ge(spare_st, 16 * SPARE)
            def step(j, s):
                wait_here(e, e_o, k * SLOTS + j - (RING - 1))
                row = nc.sync.value_load(slot_row[0:1, ds(j, 1)], min_val=0, max_val=ROWS - TILE)
                e.dma_start(XS[s], region[ds(row, TILE), :]).then_inc(e_ld[s], 16)
            stepped(nc.sync, step, 0)

        def experts_pe(e, k):
            J = k * SLOTS
            def tx(j, s):
                e.wait_ge(e_ld[s], 16 * uses(k, j, RING))
                wait(e, e_xs, J + j)
                nc.tensor.transpose(bJ[:, 0:128], XS[s][:, XN:XN + D], ident[:, :]).then_inc(e_tx, 1)
            def hidden(j, s, ex):
                e.wait_ge(e_xs, J + j + 1)
                wait(e, e_g, J + j - 1)
                s = s % 2
                hi, lo = w1s[:, 0, ds(ex * F, F)], w1s[:, 1, ds(ex * F, F)]
                nc.tensor.matmul(bS[s][:, :], XH[s][:, :], hi, start=True, stop=False)
                nc.tensor.matmul(bS[s][:, :], XH[s][:, :], lo, start=False, stop=False)
                nc.tensor.matmul(bS[s][:, :], XL[s][:, :], hi, start=False, stop=False)
                nc.tensor.matmul(bS[s][:, :], onesr[:, :], b1s[:, ds(ex * F, F)], start=False, stop=True).then_inc(e_h, 1)
            def hidden_T(j, s):
                e.wait_ge(e_g, J + j + 1)
                wait(e, e_ge, J + j - 1)
                for c in range(FC):
                    last = nc.tensor.transpose(bT[s % 2][:, 128 * c:128 * c + 128], G[s % 4][:, 128 * c:128 * c + 128],
                                               ident[:, :])
                last.then_inc(e_gt, 1)
            def down(j, s, ex):
                e.wait_ge(e_ge, J + j + 1)
                wait(e, e_o, J + j)
                for c in range(FC):
                    nc.tensor.matmul(bY[:, 0:D], GT[s % 4][:, 128 * c:128 * c + 128],
                                     w2s[:, ds(ex, 1), c, :].rearrange("p o d -> p (o d)"), start=(c == 0), stop=False)
                nc.tensor.matmul(bY[:, 0:D], onesr[:, :], b2s[:, ds(ex * D, D)], start=False, stop=True).then_inc(e_y, 1)
            tx(0, 0)
            ex = {}
            def step(j, s):
                if not isinstance(j, int) or j + 1 < SLOTS:
                    tx(j + 1, (s + 1) % RING)
                if s == 0 and tile_at(j):
                    ex[0] = expert_of(nc.tensor, j)
                if tile_at(j):
                    hidden(j, s, ex[s])
                if s < 2 and tile_at(j - 2):
                    ex[(s - 2) % RING] = expert_of(nc.tensor, j - 2)
                if tile_at(j - 1):
                    hidden_T(j - 1, (s - 1) % RING)
                if s < RING - 1 and tile_at(j + 1):
                    ex[s + 1] = expert_of(nc.tensor, j + 1)
                if tile_at(j - 2):
                    down(j - 2, (s - 2) % RING, ex[(s - 2) % RING])
            stepped(nc.tensor, step, 2)

        def experts_dve(e, k):
            J = k * SLOTS
            def split(j, s):
                e.wait_ge(e_tx, J + j + 1)
                wait(e, e_h, J + j - 1)
                nc.vector.tensor_copy(XH[s % 2][:, :], bJ[:, 0:128])
                nc.vector.drain()
                nc.vector.tensor_tensor(XL[s % 2][:, :], bJ[:, 0:128], XH[s % 2][:, :], ALU.subtract).then_inc(e_xs, 1)
            def last(j, s):
                e.wait_ge(e_y, J + j + 1)
                if k or not isinstance(j, int) or j >= 4:
                    e.wait_ge(e_sc[s % 4], 16 * (uses(k, j, 4) - 1))
                nc.vector.tensor_copy(out_tok[s % 4][:, :], XS[s][:, TOK:TOK + 1].bitcast(i32))
                nc.vector.scalar_tensor_tensor(OUT[s % 4], bY[:, 0:D], XS[s][:, GATE:GATE + 1], XS[s][:, XX:XX + D],
                                               ALU.mult, ALU.add).then_inc(e_o, 1)
            split(0, 0)
            def step(j, s):
                if not isinstance(j, int) or j + 1 < SLOTS:
                    split(j + 1, (s + 1) % RING)
                if tile_at(j - 2):
                    last(j - 2, (s - 2) % RING)
            stepped(nc.vector, step, 2)

        def experts_act(e, k, high=None):
            J = k * SLOTS
            def step(j, s):
                if high and isinstance(j, int) and 1 <= j <= NCH - EX:
                    high(EX + j - 1)
                if tile_at(j):
                    e.wait_ge(e_h, J + j + 1)
                    wait(e, e_gt, J + j - 3)
                    nc.scalar.activation(G[s % 4], bS[s % 2][:, :], ACT.Gelu_apprx_tanh).then_inc(e_g, 1)
                if tile_at(j - 1):
                    t = (s - 1) % RING
                    e.wait_ge(e_gt, J + j)
                    wait(e, e_y, J + j - 4)
                    nc.scalar.activation(GT[t % 4], bT[t % 2][:, :], ACT.Copy).then_inc(e_ge, 1)
            stepped(nc.scalar, step, 1)

        def experts_pool(e, k, dst, low=None):
            def step(j, s):
                if low and isinstance(j, int) and j < NCH - EX:
                    low(EX + j)
                wait_here(e, e_o, k * SLOTS + j + 1)
                nc.gpsimd.indirect_dma_start(
                    dst, bass.IndirectOffsetOnAxis(ap=out_tok[s % 4][:, :], axis=0), OUT[s % 4], None,
                    bounds_check=N - 1, oob_is_err=False).then_inc(e_sc[s % 4], 16)
            stepped(nc.gpsimd, step, 0)
            for s in range(4):
                e.wait_ge(e_sc[s], 16 * (SLOTS // 4) * (k + 1))

        def attention(e, body):
            def batch(b):
                for p in range(PEELED):
                    body(b, p, p % 2)
                with e.Fori(PEELED // 2, PAIRS // 2) as k:
                    for s in range(2):
                        body(b, k * 2 + s, s)
            batch(0)
            with e.Fori(1, B) as b:
                batch(b)

        def extras(b, p):
            early = isinstance(p, int)
            return early and p == 0, early and p == 1 and not isinstance(b, int), early and p == 0 and isinstance(b, int)

        def idx(b, p):
            return b * PAIRS + p

        def stacked(n, par):
            return (n - par) * 48 + 96

        def pe_proj(e, n, which, par, xbatch, to=bJ):
            if which == "k":
                e.wait_ge(ws_ld[par], (n - par) * 8 + 16)
                e.wait_ge(xb_ld, (xbatch + 1) * 16)
            o = 0 if which == "q" else 2
            W = WS[par]
            nc.tensor.matmul(to[:, :], W[:, o, :], xTb[:, 0, :], start=True, stop=False)
            nc.tensor.matmul(to[:, :], W[:, o, :], xTb[:, 1, :], start=False, stop=False)
            nc.tensor.matmul(to[:, :], W[:, o + 1, :], xTb[:, 0, :], start=False, stop=True)\
                .then_inc(s_pq if which == "q" else s_pk, 1)

        def pe_proj_v(pair, to=bJ):
            hi, lo = wvs[:, 0, ds(pair * 128, 128)], wvs[:, 1, ds(pair * 128, 128)]
            for j in range(NJ):
                o_, c = to[:, 128 * j:128 * j + 128], slice(128 * j, 128 * j + 128)
                nc.tensor.matmul(o_, xTb[:, 0, c], hi, start=True, stop=False)
                nc.tensor.matmul(o_, xTb[:, 0, c], lo, start=False, stop=False)
                last = nc.tensor.matmul(o_, xTb[:, 1, c], hi, start=False, stop=True)
            last.then_inc(s_pv, 1)

        def pe_scores(e, i, par, g):
            G_ = i * NG + g
            if g == 0:
                e.wait_ge(qk_ld[par], stacked(i, par))
            wait(e, s_exp, G_ - 2)
            h = g // 3
            S = bS[g % 3]
            for qt, c0, nb in SUPER[g % 3]:
                for part in range(2):
                    nc.tensor.matmul(S[:, c0:c0 + 128 * nb], QD[par][:, h, 128 * qt:128 * qt + 128],
                                     KD[par][:, h, part, 0:128 * nb], start=(part == 0), stop=False)
                last = nc.tensor.matmul(S[:, c0 + 128 * (nb - 1):c0 + 128 * nb], identb[:, :], maskb[:, :],
                                        start=False, stop=True)
            last.then_inc(s_S, 1)

        def pe_PT(e, i, g):
            G_ = i * NG + g
            e.wait_ge(s_exp, G_ + 1)
            wait(e, s_pt, G_ - 1)
            w = sum(nb for _, _, nb in SUPER[g % 3])
            for c in range(w):
                last = nc.tensor.transpose(bT[g % 2][:, 128 * c:128 * c + 128], P[g % 3][:, 128 * c:128 * c + 128], ident[:, :])
            last.then_inc(s_T, 1)

        def pe_AV(e, i, par, g):
            G_ = i * NG + g
            e.wait_ge(s_pt, G_ + 1)
            if g == 0:
                e.wait_ge(s_vr, i + 1)
                wait(e, s_norm, i)
            hh = g // 3
            for qt, c0, nb in SUPER[g % 3]:
                u = 4 * hh + qt
                for kb in range(nb):
                    last = nc.tensor.matmul(bO[:, DH * u:DH * u + DH], PT[g % 2][:, c0 + 128 * kb:c0 + 128 * kb + 128],
                                            V[par][:, kb, DH * hh:DH * hh + DH], start=(kb == 0), stop=(kb == nb - 1))
            last.then_inc(s_av, 1)

        def pe_OT(e, i, par):
            e.wait_ge(s_norm, i + 1)
            for j in range(NJ):
                last = nc.tensor.transpose(bJ[:, 128 * j:128 * j + 128], O[par][:, j, :, :].rearrange("p h d -> p (h d)"), ident[:, :])
            last.then_inc(s_ot, 1)

        def pe_Wo(e, i, pair, batch, final):
            e.wait_ge(s_ote, i + 1)
            first_ = isinstance(pair, int) and pair == 0
            if first_:
                wait(e, s_x2, batch)
            for j in range(NJ):
                last = nc.tensor.matmul(bY[:, 128 * j:128 * j + 128], OT[:, 128 * j:128 * j + 128],
                                        wos[:, ds(pair, 1), :].rearrange("p o d -> p (o d)"),
                                        start=(first_ and j == 0), stop=final, skip_group_check=True)
            last.then_inc(s_wo, 1)

        def pe_prepare(e, m):
            e.wait_ge(l_xn, m + 1)
            pe_norm_T(1, bJ, l_t)

        def pe_attention(e):
            def body(b, p, s):
                i = idx(b, p)
                n = i + 1
                par, npar = s, 1 - s
                prepare, router, first = extras(b, p)
                busy = prepare or (isinstance(p, int) and p == 1)
                pe_scores(e, i, par, 2)
                pe_PT(e, i, 0)
                e.wait_ge(s_qr, n + 1)
                pe_proj_v((p + 1) % PAIRS)
                pe_scores(e, i, par, 3)
                if s == 0 and not prepare:
                    e.wait_ge(r_rkr, b + 8)
                pe_PT(e, i, 1)
                pe_AV(e, i, par, 0)
                pe_scores(e, i, par, 4)
                e.wait_ge(s_vr, n + 1)
                if not first:
                    pe_OT(e, i - 1, npar)
                pe_PT(e, i, 2)
                pe_AV(e, i, par, 1)
                pe_scores(e, i, par, 5)
                pe_PT(e, i, 3)
                if not first:
                    pe_Wo(e, i - 1, PAIRS - 1 if prepare else p - 1, b, prepare)
                if prepare:
                    pe_prepare(e, b + 1)
                if router:
                    e.wait_ge(r_xn, b + 8)
                    pe_norm_T(0, bJ, r_t)
                pe_AV(e, i, par, 2)
                if not busy:
                    e.wait_ge(s_ote, i)
                    pe_proj(e, n + 1, "k", par, b + (p + 2) // PAIRS)
                pe_scores(e, n, npar, 0)
                pe_PT(e, i, 4)
                if router:
                    pe_logits(e, b + 7, bJ)
                pe_AV(e, i, par, 3)
                if prepare:
                    e.wait_ge(l_lo, b + 2)
                if router:
                    e.wait_ge(r_d, b + 8)
                if busy:
                    pe_proj(e, n + 1, "k", par, b + (p + 2) // PAIRS)
                else:
                    e.wait_ge(s_kr, n + 2)
                    pe_proj(e, n + 1, "q", par, None)
                pe_scores(e, n, npar, 1)
                pe_PT(e, i, 5)
                pe_AV(e, i, par, 4)
                if busy:
                    e.wait_ge(s_kr, n + 2)
                    pe_proj(e, n + 1, "q", par, None)
                pe_AV(e, i, par, 5)
                if router:
                    pe_rank(e, b + 7, bT[1])
            pe_prepare(e, 0)
            e.wait_ge(l_lo, 1)
            pe_proj(e, 0, "k", 0, 0, to=bS[2])
            pe_proj(e, 0, "q", 0, None, to=bT[0])
            pe_proj_v(0, to=bY)
            pe_proj(e, 1, "k", 1, 0, to=bT[1])
            pe_proj(e, 1, "q", 1, None, to=bO)
            pe_scores(e, 0, 0, 0)
            pe_scores(e, 0, 0, 1)
            e.wait_ge(s_qr, 2)
            attention(nc.tensor, body)
            i = B * PAIRS - 1
            e.wait_ge(s_qr, i + 3)
            pe_OT(e, i, 1)
            pe_Wo(e, i, PAIRS - 1, B, True)
            e.wait_ge(r_xn, 8 + B)
            pe_norm_T(0, bJ, r_t)
            pe_logits(e, B + 7, bJ)
            pe_rank(e, B + 7, bT[1])

        def dve_max(e, i, par, g):
            e.wait_ge(s_S, i * NG + g + 1)
            for qt, c0, nb in SUPER[g % 3]:
                u = 4 * (g // 3) + qt
                last = nc.vector.tensor_reduce(nmax[par][:, u:u + 1], bS[g % 3][:, c0:c0 + 128 * nb], AX.X, ALU.max, negate=True)
            last.then_inc(s_max, 1)

        swap = [c ^ 1 for c in range(32)]

        def dve_rope(e, n, which, src=bJ):
            done, free, read = (s_pq, s_qt, s_qr) if which == "q" else (s_pk, s_kt, s_kr)
            C_, S_, o = (cosq, sinq, 0) if which == "q" else (cosk, sink, 2)
            e.wait_ge(done, n + 1)
            wait(e, free, n)
            nc.vector.tensor_tensor(C_[:, :], src[:, :], rope[:, o, :], ALU.mult)
            nc.vector.stream_shuffle(S_[:, :], src[:, :], mask=swap).then_inc(read, 1)

        def halves():
            return ((0, slice(0, DH), slice(DH, 128)), (1, slice(DH, 128), slice(0, DH)))

        def dve_k_low(e, n, par):
            e.wait_ge(s_kh, n + 1)
            for h, own, _ in halves():
                last = nc.vector.tensor_tensor(KD[par][own, h, 1, :], RK[own, :], KD[par][own, h, 0, :], ALU.subtract)
            last.then_inc(s_kl, 1)

        def dve_x2(e, b1_):
            e.wait_ge(s_wo, b1_ * PAIRS)
            e.wait_ge(s_bo, b1_)
            x_ = PL[0][:, :, XX:XX + D]
            nc.vector.tensor_tensor(x_, bY[:, :].rearrange("p (j d) -> p j d", j=NJ), x_, ALU.add).then_inc(s_x2, 1)
            nc.vector.drain()
            dve_stats(0)
            dve_var(for_router)

        def dve_low(e, m, dst=xTn):
            e.wait_ge(l_hi, m + 1)
            nc.vector.tensor_tensor(dst[:, 1, :], bJ[:, :], dst[:, 0, :], ALU.subtract).then_inc(l_lo, 1)

        def dve_attention(e):
            def norm(i, par):
                e.wait_ge(s_av, i * NG + NG)
                nc.vector.reciprocal(rinv[:, :], rsum[par][:, :])
                nc.vector.drain()
                nc.vector.tensor_tensor(O[par][:, :, :, :].rearrange("p j h d -> p h j d"),
                                        bO[:, :].rearrange("p (h j d) -> p h j d", h=2, j=NJ),
                                        rinv[:, :].rearrange("p (h j) -> p h j", h=2).unsqueeze(3).broadcast_to([128, 2, NJ, DH]),
                                        ALU.mult).then_inc(s_norm, 1)
            def body(b, p, s):
                i = idx(b, p)
                n = i + 1
                par, npar = s, 1 - s
                prepare, router, first = extras(b, p)
                busy = prepare or (isinstance(p, int) and p == 1)
                dve_max(e, i, par, 2)
                dve_k_low(e, n, npar)
                if router:
                    dve_x2(e, b)
                dve_max(e, i, par, 3)
                if prepare:
                    e.wait_ge(x_ld[1], (b + 3) * 16)
                    dve_stats(1)
                    dve_var(for_attention)
                dve_max(e, i, par, 4)
                if prepare:
                    dve_norm(e, b + 1, 1, for_attention)
                if router:
                    dve_norm(e, b + LN_AFTER, 0, for_router)
                dve_max(e, i, par, 5)
                if prepare:
                    dve_low(e, b + 1)
                if not busy:
                    dve_rope(e, n + 1, "k")
                dve_max(e, n, npar, 0)
                if router:
                    dve_route(e, b + 7, bJ)
                dve_rope(e, n + 1, "k" if busy else "q")
                dve_max(e, n, npar, 1)
                if busy:
                    dve_rope(e, n + 1, "q")
                norm(i, par)
                if router:
                    dve_position(e, b + 7, b - 1, 0, bT[1])
            e.wait_ge(x_ld[1], 32)
            dve_stats(1)
            dve_var(for_attention)
            dve_norm(e, 0, 1, for_attention)
            dve_low(e, 0, xTb)
            dve_rope(e, 0, "k", src=bS[2])
            dve_rope(e, 0, "q", src=bT[0])
            dve_k_low(e, 0, 0)
            dve_rope(e, 1, "k", src=bT[1])
            dve_rope(e, 1, "q", src=bO)
            dve_max(e, 0, 0, 0)
            dve_max(e, 0, 0, 1)
            attention(nc.vector, body)
            dve_x2(e, B)
            dve_norm(e, B + LN_AFTER, 0, for_router)
            dve_route(e, B + 7, bJ)
            dve_position(e, B + 7, B - 1, 0, bT[1])

        def act_attention(e):
            def exps(i, par, g):
                G_ = i * NG + g
                e.wait_ge(s_max, G_ + 1)
                wait(e, s_T, G_ - 2)
                for qt, c0, nb in SUPER[g % 3]:
                    u = 4 * (g // 3) + qt
                    last = nc.scalar.activation(P[g % 3][:, c0:c0 + 128 * nb], bS[g % 3][:, c0:c0 + 128 * nb], ACT.Exp,
                                                bias=nmax[par][:, u:u + 1], accum_out=rsum[par][:, u:u + 1])
                last.then_inc(s_exp, 1)
            def pt_out(i, g):
                G_ = i * NG + g
                e.wait_ge(s_T, G_ + 1)
                wait(e, s_av, G_ - 1)
                w = 128 * sum(nb for _, _, nb in SUPER[g % 3])
                nc.scalar.activation(PT[g % 2][:, 0:w], bT[g % 2][:, 0:w], ACT.Copy).then_inc(s_pt, 1)
            def v_out(n, par, src=bJ):
                e.wait_ge(s_pv, n + 1)
                wait(e, s_av, (n - 1) * NG)
                nc.scalar.activation(V[par][:, :, :], src[:, :].rearrange("p (j d) -> p j d", j=NJ), ACT.Copy).then_inc(s_vr, 1)
            def ot_out(i):
                e.wait_ge(s_ot, i + 1)
                wait(e, s_wo, i)
                nc.scalar.activation(OT[:, :], bJ[:, :], ACT.Copy).then_inc(s_ote, 1)
            def high_(m, dst=xTn):
                e.wait_ge(l_t, m + 1)
                wait(e, xb_ld, m * 16)
                nc.scalar.activation(dst[:, 0, :], bJ[:, :], ACT.Copy).then_inc(l_hi, 1)
            def k_high(n, par):
                e.wait_ge(s_kt, n + 1)
                wait(e, s_S, (n - 1) * NG)
                for h, own, _ in halves():
                    last = nc.scalar.activation(KD[par][own, h, 0, :], RK[own, :], ACT.Copy)
                last.then_inc(s_kh, 1)
            def q_high(n, par):
                e.wait_ge(s_qt, n + 1)
                if not isinstance(n, int) or n > 0:
                    e.wait_ge(qk_ld[1 - par], stacked(n - 1, 1 - par))
                nc.scalar.activation(QH, RQ[:, :], ACT.Copy).then_inc(s_qh, 1)
            def body(b, p, s):
                i = idx(b, p)
                n = i + 1
                par, npar = s, 1 - s
                prepare, router, first = extras(b, p)
                k_high(n, npar)
                for g in range(NG):
                    if g < NG - 1:
                        exps(i, par, g + 1)
                    else:
                        exps(n, npar, 0)
                    pt_out(i, g)
                    if g == 0:
                        q_high(n, npar)
                        v_out(n, npar)
                    if g == 1 and not first:
                        ot_out(i - 1)
                    if g == 3 and prepare:
                        high_(b + 1)
                    if g == 3 and router:
                        act_xT(e, b + 7, bJ)
                    if g == 5 and router:
                        act_exp(e, b + 7)
            high_(0, xTb)
            k_high(0, 0)
            v_out(0, 0, bY)
            q_high(0, 0)
            exps(0, 0, 0)
            attention(nc.scalar, body)
            ot_out(B * PAIRS - 1)
            act_xT(e, B + 7, bJ)
            act_exp(e, B + 7)

        def pool_attention(e):
            def add(n, which):
                parts, done, R, used, C_, S_, o = (s_qr, s_qt, RQ, s_ql, cosq, sinq, 0) if which == "q" else \
                    (s_kr, s_kt, RK, s_kl, cosk, sink, 2)
                e.wait_ge(parts, n + 1)
                nc.gpsimd.tensor_tensor(S_[:, :], S_[:, :], rope[:, o + 1, :], ALU.mult)
                e.drain()
                wait(e, used, n)
                nc.gpsimd.tensor_tensor(R[:, :], C_[:, :], S_[:, :], ALU.add).then_inc(done, 1)
            def q_low(n, par):
                e.wait_ge(s_qh, n + 1)
                nc.gpsimd.tensor_tensor(QL, RQ[:, :], QH, ALU.subtract).then_inc(s_ql, 1)
            def bias(b):
                e.wait_ge(x_ld[0], (b + 2) * 16)
                for j in range(NJ):
                    last = nc.gpsimd.tensor_tensor(PL[0][:, j, XX:XX + D], PL[0][:, j, XX:XX + D], bo_bc[:, :], ALU.add)
                last.then_inc(s_bo, 1)
            def body(b, p, s):
                i = idx(b, p)
                prepare, router, first = extras(b, p)
                q_low(i + 1, 1 - s)
                if isinstance(p, int) and p == 2 and not isinstance(b, int):
                    pool_scatter(e, b + 7, 0)
                if prepare:
                    pool_rstd(e, b + 1, for_attention)
                    if not isinstance(b, int):
                        bias(b - 1)
                if router:
                    pool_rstd(e, b + LN_AFTER, for_router)
                add(i + 2, "k")
                add(i + 2, "q")
            pool_rstd(e, 0, for_attention)
            add(0, "k")
            add(0, "q")
            q_low(0, 0)
            add(1, "k")
            add(1, "q")
            attention(nc.gpsimd, body)
            bias(B - 1)
            pool_rstd(e, B + LN_AFTER, for_router)
            pool_scatter(e, B + 7, 0)

        def sp_attention(e):
            def load_w(n, par, pair):
                wait_here(e, s_pq, n - 1)
                e.dma_start(WS[par][:, :, :].bitcast(f32), wqk[:, :, ds(pair * 128, 128)].bitcast(f32)).then_inc(ws_ld[par], 16)
            def next_x(m):
                wait_here(e, s_pv, m * PAIRS)
                wait_here(e, l_lo, m + 1)
                e.dma_start(xTb[:, :, :].bitcast(f32), xTn[:, :, :].bitcast(f32)).then_inc(xb_ld, 16)
            def tokens_of(m, batch):
                wait_here(e, l_t, m)
                e.dma_start(PL[1][:, :, XX:XX + D], xrows(x1, batch)).then_inc(x_ld[1], 16)
            def residual(b):
                wait_here(e, r_sc[0], (b + 1) * 64)
                e.dma_start(PL[0][:, :, XX:XX + D], xrows(x1, b)).then_inc(x_ld[0], 16)
            def stack_k(n, par):
                wait_here(e, s_kl, n + 1)
                for h, own, other in halves():
                    e.dma_start(KD[par][other, h, :, :].bitcast(f32), KD[par][own, h, :, :].bitcast(f32)).then_inc(qk_ld[par], 16)
            def stack_q(n, par):
                wait_here(e, s_ql, n + 1)
                if not isinstance(n, int) or n > 1:
                    wait_here(e, s_S, (n - 1) * NG)
                for h, own, other in halves():
                    for at, part in ((own, QH), (other, QL)):
                        e.dma_start(QD[par][at, h, :].bitcast(f32), part[own, :].bitcast(f32)).then_inc(qk_ld[par], 16)
            def body(b, p, s, middle=None):
                i = idx(b, p)
                stack_k(i + 1, 1 - s)
                if middle:
                    middle()
                stack_q(i + 1, 1 - s)
                load_w(i + 3, 1 - s, (p + 3) % PAIRS)
            def batch(b):
                tokens_of(b + 1, (b + 1) % B)
                if not isinstance(b, int):
                    residual(b - 1)
                for s in range(2):
                    body(b, s, s)
                with nc.sync.Fori(1, PAIRS // 2 - 1) as k:
                    for s in range(2):
                        body(b, k * 2 + s, s)
                body(b, PAIRS - 2, 0, lambda: next_x(b + 1))
                body(b, PAIRS - 1, 1)
            tokens_of(0, 0)
            load_w(0, 0, 0)
            load_w(1, 1, 1)
            wait_here(e, l_lo, 1)
            e.sem_inc(xb_ld, 16)
            stack_k(0, 0)
            stack_q(0, 0)
            load_w(2, 0, 2)
            batch(0)
            with nc.sync.Fori(1, B) as b:
                batch(b)
            residual(B - 1)

        block = ctx.enter_context(nc.Block())

        @block.sync
        def _(sp):
            def tokens_in(b):
                sp.dma_start(PL[b][:, :, XX:XX + D], xrows(x, b)).then_inc(x_ld[b], 16)
            tokens_in(0)
            sp.dma_start(ident[:], c_ident).then_inc(c_ld, 16)
            tokens_in(1)
            sp.dma_start(swt[:], sw).then_inc(c_ld, 16)
            tokens_in(2)
            sp.dma_start(small[:], c_small).then_inc(c_ld, 16)
            tokens_in(3)
            sp.dma_start(sbias[:], sb_.rearrange("(o j e) -> o j e", o=1, j=1).broadcast_to([128, NJ, EX])).then_inc(c_ld, 16)
            for b in range(4, B):
                tokens_in(b)
            for dst, src in ((slot_c, c_slots), (bo_bc, bo.rearrange("(o d) -> o d", o=1).broadcast_to([128, D])),
                             (rope, c_rope)):
                sp.dma_start(dst[:], src).then_inc(c_ld2, 16)
            sp.wait_ge(prep, 1)
            for s_ in range(SPARE):
                r0 = EX * REGION + s_ * TILE
                sp.dma_start(region[r0:r0 + TILE, :], pad[:, :]).then_inc(spare_st, 16)
            pads(sp, nc.sync, 0, range(0, EX, 2))
            experts_sp(sp, 0, [64] * NPL)
            all_meet(sp, 1)
            sp_attention(sp)
            pads(sp, nc.sync, 1, range(0, EX, 2))
            all_meet(sp, 2)
            experts_sp(sp, 1, [64 * (1 + B)] + [64] * (NPL - 1))
            all_meet(sp, 3)

        @block.scalar
        def _(act):
            act.dma_start(bias_raw[:, 0:32], b1.rearrange("e (a c) -> (e a) c", c=32)).then_inc(bias_in, 16)
            act.dma_start(bias_raw[:, 32:40], b2.rearrange("e (a c) -> (e a) c", c=8)).then_inc(bias_in, 16)
            for c in range(NRAW):
                act.dma_start(raw[c][:, :], chunks[c][0]).then_inc(raw_ld[c], 16)
            def high(c):
                act.wait_ge(raw_ld[c % NRAW], 16 * (c // NRAW + 1))
                nc.scalar.activation(chunks[c][1], raw[c % NRAW][:, :], ACT.Copy).then_inc(raw_hi, 1)
                new = c + NRAW - 1
                if NRAW <= new < NCH:
                    act.wait_ge(raw_lo, c)
                    act.dma_start(raw[new % NRAW][:, :], chunks[new][0]).then_inc(raw_ld[new % NRAW], 16)
            act.wait_ge(bias_in, 32)
            nc.scalar.activation(bias_hl[:, 0, :], bias_raw[:, :], ACT.Copy).then_inc(bias_hi, 1)
            high(0)
            act_xT(act, 0, bJ)
            for b in range(B):
                if b + 1 < B:
                    act_xT(act, b + 1, bJ)
                act_exp(act, b)
                if b == 1:
                    act.dma_start(w2s[:, :, :, :], w2.rearrange("e (c p) d -> p e c d", p=128)).then_inc(w2_ld, 16)
                    act.dma_start(wos[:, :, :], wo.rearrange("(a p) d -> p a d", p=128)).then_inc(w2_ld, 16)
                if b + 1 < EX:
                    high(b + 1)
            pads(act, nc.scalar, 0, range(1, EX, 2))
            experts_act(act, 0, high)
            all_meet(act, 1)
            act_attention(act)
            pads(act, nc.scalar, 1, range(1, EX, 2))
            all_meet(act, 2)
            experts_act(act, 1)
            all_meet(act, 3)

        @block.gpsimd
        def _(pool):
            nc.gpsimd.memset(pad[:, :], 0.0)
            pool.drain()
            nc.gpsimd.memset(pad[:, TOK:TOK + 1].bitcast(i32), NOWHERE)
            nc.gpsimd.iota(tokens[:, :], [[TILE, N // TILE]], base=0, channel_multiplier=1)
            nc.gpsimd.memset(onesb[:, :], 1.0)
            nc.gpsimd.memset(mhalf[:, :], -0.5)
            nc.gpsimd.memset(onesr[:, :].bitcast(f32), 1.0)
            pool.drain().then_inc(prep, 1)
            nc.gpsimd.dma_start(upperb[:, :], c_upper).then_inc(bf_ld, 16)
            nc.gpsimd.dma_start(identb[:, :], c_ident).then_inc(bf_ld, 16)
            nc.gpsimd.dma_start(maskb[:, :], c_mask).then_inc(bf_ld, 16)
            for m in range(len(LN) - 1):
                pool_rstd(pool, m, for_router, LN[m], LN[m + 1])
            pool.wait_ge(bias_hi, 1)
            nc.gpsimd.tensor_tensor(bias_hl[:, 1, :], bias_raw[:, :], bias_hl[:, 0, :], ALU.subtract)
            pool.drain()
            for r in range(2):
                nc.gpsimd.dma_start(b1s[r:r + 1, :].rearrange("o (a c) -> o a c", c=32).bitcast(f32), bias_hl[:, r, 0:32].bitcast(f32)).then_inc(bias_ld, 16)
                nc.gpsimd.dma_start(b2s[r:r + 1, :].rearrange("o (a c) -> o a c", c=8).bitcast(f32), bias_hl[:, r, 32:40].bitcast(f32)).then_inc(bias_ld, 16)
            def low(c):
                pool.wait_ge(raw_hi, c + 1)
                nc.gpsimd.tensor_tensor(chunks[c][2], raw[c % NRAW][:, :], chunks[c][1], ALU.subtract).then_inc(raw_lo, 1)
            for b in range(B):
                low(b)
                pool_scatter(pool, b, b % NPL)
            experts_pool(pool, 0, x1, low)
            all_meet(pool, 1)
            pool.wait_ge(c_ld2, 48)
            pool_attention(pool)
            all_meet(pool, 2)
            experts_pool(pool, 1, out)
            all_meet(pool, 3)

        @block.vector
        def _(dve):
            nc.vector.memset(cum[:, :], 0.0)
            def stats_of(m):
                for b in range(LN[m], LN[m + 1]):
                    dve.wait_ge(x_ld[b], 16)
                    dve_stats(b, b)
                dve_var(for_router, LN[m], LN[m + 1])
            def norm_of(b):
                m = sum(b >= at for at in LN) - 1
                dve_norm(dve, m, b, for_router, b)
            stats_of(0)
            stats_of(1)
            norm_of(0)
            norm_of(1)
            stats_of(2)
            dve.wait_ge(c_ld, 64)
            dve.wait_ge(prep, 1)
            for b in range(B):
                dve_route(dve, b, bS[b % 2])
                if b + 2 < B:
                    norm_of(b + 2)
                dve_position(dve, b, b, b % NPL, bO)
            dve.wait_ge(c_ld2, 48)
            dve.drain()
            dve_table(dve, 0)
            experts_dve(dve, 0)
            all_meet(dve, 1)
            nc.vector.memset(cum[:, :], 0.0)
            dve_attention(dve)
            dve.drain()
            dve_table(dve, 1)
            all_meet(dve, 2)
            experts_dve(dve, 1)
            all_meet(dve, 3)

        @block.tensor
        def _(pe):
            pe.wait_ge(c_ld, 64)
            def logits_of(b):
                pe.wait_ge(r_xn, b + 1)
                wait(pe, r_xt, b)
                pe_norm_T(b % NPL, bJ, r_t)
                pe_logits(pe, b, bS[b % 2])
            logits_of(0)
            pe.wait_ge(bf_ld, 48)
            pe.wait_ge(prep, 1)
            for b in range(B):
                if b + 1 < B:
                    logits_of(b + 1)
                pe_rank(pe, b, bO)
            pe_counts(pe, 0)
            pe.wait_ge(r_tab, 1)
            pe.wait_ge(bias_ld, 64)
            pe.wait_ge(raw_lo, EX)
            pe.wait_ge(w2_ld, 32)
            experts_pe(pe, 0)
            all_meet(pe, 1)
            pe.wait_ge(raw_lo, NCH)
            pe_attention(pe)
            pe_counts(pe, 1)
            all_meet(pe, 2)
            experts_pe(pe, 1)
            all_meet(pe, 3)


_INS = ["L0_attn_x", "L0_attn_Wq", "L0_attn_Wk", "L0_attn_Wv", "L0_attn_Wo", "L0_attn_bo",
        "L0_ffn_switch_w", "L0_ffn_switch_b", "L0_ffn_w1", "L0_ffn_b1", "L0_ffn_w2", "L0_ffn_b2"]


def _constants():
    f = np.float32
    p = np.arange(128)
    inv = (1.0 / 10000.0 ** (np.arange(0, DH, 2, dtype=f) / f(DH))).astype(f)
    ang = (np.arange(T, dtype=f)[:, None] * inv[None, :]).astype(f)
    cos = np.cos(ang).astype(f)[:, (p % DH) // 2].T
    sin = np.sin(ang).astype(f)[:, (p % DH) // 2].T * np.where(p % 2 == 0, -1, 1)[:, None].astype(f)
    scale = f(DH ** -0.5)
    rope = np.stack([cos * scale, sin * scale, cos, sin], 1).astype(f)
    e = np.arange(EX, dtype=f)
    small = np.zeros((128, 2, NJ, EX), f)
    small[:, 0], small[:, 1] = EX - e, e * REGION
    s = np.arange(SLOTS, dtype=f)
    slots = np.concatenate([s * TILE, np.repeat(s, EX), (e[None, :] <= e[:, None]).astype(f).ravel(),
                            np.tile(np.arange(32, dtype=f) * TILE, EX)])[None]
    return {
        "ident": np.eye(128, dtype=f),
        "mask": np.where(p[None, :] > p[:, None], MASKED, 0).astype(f),
        "upper": (p[:, None] < p[None, :]).astype(f),
        "rope": rope, "small": small, "slots": slots.astype(f),
    }


def kernel(**inputs):
    import concourse.bacc as _bacc
    from concourse.bass_utils import run_bass_kernel_spmd as _run

    nc = _bacc.Bacc("TRN2", target_bir_lowering=False, num_devices=1)
    arrays, args = {}, []

    def given(name, a):
        a = np.ascontiguousarray(a)
        arrays[name] = a
        args.append(nc.dram_tensor(name, a.shape, mybir.dt.from_np(a.dtype), kind="ExternalInput").ap())

    for name in _INS:
        a = np.asarray(inputs[name])
        if name == "L0_attn_x":
            a = a.reshape(N, D)
        given(f"in_{name}", a)
    for name, a in _constants().items():
        given(f"const_{name}", a)
    out = nc.dram_tensor("out_0", (N, D), mybir.dt.float32, kind="ExternalOutput").ap()
    macaron_kernel(nc, *args, out)
    r = _run(nc, [arrays], core_ids=[0])
    return np.asarray(r.results[0]["out_0"]).reshape(B, T, D)
```
